# Optimizing a Trainium2 kernel written in Bass

```python
import numpy as np
import jax
import jax.numpy as jnp

def _softmax(x, axis=-1):
    return jax.nn.softmax(x, axis=axis)

def _gelu(x):
    return jax.nn.gelu(x, approximate=True)

def _silu(x):
    return jax.nn.silu(x)

def _sigmoid(x):
    return jax.nn.sigmoid(x)

def _layernorm(x, axis=-1, eps=1e-05):
    m = jnp.mean(x, axis=axis, keepdims=True)
    v = jnp.var(x, axis=axis, keepdims=True)
    return (x - m) / jnp.sqrt(v + eps)

def _scatter_add(tgt, idx, src, axis=0):
    return tgt.at[idx].add(src)

def _segment_sum(src, seg, n):
    return jax.ops.segment_sum(src, seg, n)
kernel_name = 'mk_adaln_d1_jaxref_r8_2581e8'

def setup_inputs(seed: int=0):
    np.random.seed(seed)
    _w = jnp.asarray

    def _L0_attn_setup():
        import jax, jax.numpy as jnp
        import numpy as np
        B, N, C, H = (4, 1024, 128, 16)
        D = C // H
        EPS = 1e-05
        key = jax.random.key(seed)
        ks = jax.random.split(key, 10)
        s = 1.0 / np.sqrt(C)
        return {'x': jax.random.normal(ks[0], (B, N, C), jnp.float32), 'Wq': jax.random.uniform(ks[1], (C, C), jnp.float32, -s, s), 'bq': jax.random.uniform(ks[2], (C,), jnp.float32, -s, s), 'Wk': jax.random.uniform(ks[3], (C, C), jnp.float32, -s, s), 'bk': jax.random.uniform(ks[4], (C,), jnp.float32, -s, s), 'Wv': jax.random.uniform(ks[5], (C, C), jnp.float32, -s, s), 'bv': jax.random.uniform(ks[6], (C,), jnp.float32, -s, s), 'Wo': jax.random.uniform(ks[7], (C, C), jnp.float32, -s, s), 'bo': jax.random.uniform(ks[8], (C,), jnp.float32, -s, s), 'ln_g': jnp.ones((C,), jnp.float32), 'ln_b': jnp.zeros((C,), jnp.float32)}
    _L0_attn_in = _L0_attn_setup()

    def _L0_ffn_setup():
        import jax, jax.numpy as jnp
        import numpy as np
        D, H, E, K = (128, 128, 8, 2)

        def _moe(x, router_w, w_in, b_in, w_out, b_out):
            B, S, Dm = x.shape
            T = B * S
            x2 = x.reshape(T, Dm)
            logits = x2 @ router_w
            probs = jax.nn.softmax(logits, axis=-1)
            top_p, top_e = jax.lax.top_k(probs, K)
            flat_e = top_e.reshape(-1)
            flat_p = top_p.reshape(-1)
            tok = jnp.repeat(jnp.arange(T), K)
            order = jnp.argsort(flat_e)
            se, sp, st = (flat_e[order], flat_p[order], tok[order])
            xd = x2[st]
            N = xd.shape[0]
            h = jnp.zeros((N, H), x.dtype)
            for e in range(E):
                m = (se == e)[:, None]
                h = h + jnp.where(m, jax.nn.gelu(xd @ w_in[e] + b_in[e]), 0.0)
            y = jnp.zeros((N, Dm), x.dtype)
            for e in range(E):
                m = (se == e)[:, None]
                y = y + jnp.where(m, h @ w_out[e] + b_out[e], 0.0)
            y = y * sp[:, None]
            out = jnp.zeros((T, Dm), x.dtype).at[st].add(y)
            return out.reshape(B, S, Dm)
        key = jax.random.key(seed)
        ks = jax.random.split(key, 5)
        s = lambda k, shape, scale: jax.random.normal(k, shape, dtype=jnp.float32) * scale
        return {'input_batch': s(ks[0], (2, 64, D), 1.0), 'router_w': s(ks[1], (D, E), D ** (-0.5)), 'w_in': s(ks[2], (E, D, H), D ** (-0.5)), 'b_in': jnp.zeros((E, H), jnp.float32), 'w_out': s(ks[3], (E, H, D), H ** (-0.5)), 'b_out': jnp.zeros((E, D), jnp.float32)}
    _L0_ffn_in = _L0_ffn_setup()
    _L0_c = _w((lambda *s: np.random.randn(*s).astype(np.float32) * 0.05)(16, 128))
    _L0_wmod = _w((lambda *s: np.random.randn(*s).astype(np.float32) * 0.05)(128, 6 * 128) * 128 ** (-0.5))
    _d = {'L0_attn_x': _L0_attn_in['x'], 'L0_attn_Wq': _L0_attn_in['Wq'], 'L0_attn_bq': _L0_attn_in['bq'], 'L0_attn_Wk': _L0_attn_in['Wk'], 'L0_attn_bk': _L0_attn_in['bk'], 'L0_attn_Wv': _L0_attn_in['Wv'], 'L0_attn_bv': _L0_attn_in['bv'], 'L0_attn_Wo': _L0_attn_in['Wo'], 'L0_attn_bo': _L0_attn_in['bo'], 'L0_attn_ln_g': _L0_attn_in['ln_g'], 'L0_attn_ln_b': _L0_attn_in['ln_b'], 'L0_ffn_router_w': _L0_ffn_in['router_w'], 'L0_ffn_w_in': _L0_ffn_in['w_in'], 'L0_ffn_b_in': _L0_ffn_in['b_in'], 'L0_ffn_w_out': _L0_ffn_in['w_out'], 'L0_ffn_b_out': _L0_ffn_in['b_out'], 'L0_c': _L0_c, 'L0_wmod': _L0_wmod}
    _x0 = _d['L0_attn_x']
    _d['L0_attn_x'] = jax.random.normal(jax.random.fold_in(jax.random.key(seed), 1), (16, 512, 128), dtype=_x0.dtype)
    del _x0
    return _d

def reference(L0_attn_x, L0_attn_Wq, L0_attn_bq, L0_attn_Wk, L0_attn_bk, L0_attn_Wv, L0_attn_bv, L0_attn_Wo, L0_attn_bo, L0_attn_ln_g, L0_attn_ln_b, L0_ffn_router_w, L0_ffn_w_in, L0_ffn_b_in, L0_ffn_w_out, L0_ffn_b_out, L0_c, L0_wmod):

    def _L0_attn_ref(x, Wq, bq, Wk, bk, Wv, bv, Wo, bo, ln_g, ln_b):
        import jax, jax.numpy as jnp
        import numpy as np
        B, N, C, H = (4, 1024, 128, 16)
        D = C // H
        EPS = 1e-05
        b, n, c = x.shape
        q = x @ Wq.T + bq
        k = x @ Wk.T + bk
        v = x @ Wv.T + bv
        split = lambda z: z.reshape(b, n, H, D).transpose(0, 2, 1, 3)
        q, k, v = (split(q), split(k), split(v))
        q = jax.nn.softmax(q, axis=-1)
        k = jax.nn.softmax(k, axis=-2)
        state = jnp.einsum('bhnd,bhne->bhde', k, v)
        out = jnp.einsum('bhnd,bhde->bhne', q, state)
        out = out.transpose(0, 2, 1, 3).reshape(b, n, c)
        mu = out.mean(-1, keepdims=True)
        var = out.var(-1, keepdims=True)
        out = (out - mu) * jax.lax.rsqrt(var + EPS) * ln_g + ln_b
        return out @ Wo.T + bo

    def _L0_ffn_ref(input_batch, router_w, w_in, b_in, w_out, b_out):
        import jax, jax.numpy as jnp
        import numpy as np
        D, H, E, K = (128, 128, 8, 2)

        def _moe(x, router_w, w_in, b_in, w_out, b_out):
            B, S, Dm = x.shape
            T = B * S
            x2 = x.reshape(T, Dm)
            logits = x2 @ router_w
            probs = jax.nn.softmax(logits, axis=-1)
            top_p, top_e = jax.lax.top_k(probs, K)
            flat_e = top_e.reshape(-1)
            flat_p = top_p.reshape(-1)
            tok = jnp.repeat(jnp.arange(T), K)
            order = jnp.argsort(flat_e)
            se, sp, st = (flat_e[order], flat_p[order], tok[order])
            xd = x2[st]
            N = xd.shape[0]
            h = jnp.zeros((N, H), x.dtype)
            for e in range(E):
                m = (se == e)[:, None]
                h = h + jnp.where(m, jax.nn.gelu(xd @ w_in[e] + b_in[e]), 0.0)
            y = jnp.zeros((N, Dm), x.dtype)
            for e in range(E):
                m = (se == e)[:, None]
                y = y + jnp.where(m, h @ w_out[e] + b_out[e], 0.0)
            y = y * sp[:, None]
            out = jnp.zeros((T, Dm), x.dtype).at[st].add(y)
            return out.reshape(B, S, Dm)
        return _moe(input_batch, router_w, w_in, b_in, w_out, b_out)
    x = L0_attn_x
    mod = (_silu(L0_c) @ L0_wmod).reshape(L0_c.shape[0], 6, 1, -1)
    sa, ca, ga, sb, cb, gb = (mod[:, 0], mod[:, 1], mod[:, 2], mod[:, 3], mod[:, 4], mod[:, 5])
    ga = (2 * (ga >= 0) - 1) * jnp.maximum(jnp.abs(ga), 0.25)
    gb = (2 * (gb >= 0) - 1) * jnp.maximum(jnp.abs(gb), 0.25)
    h = _layernorm(x, axis=-1) * (1 + ca) + sa
    x = x + ga * _L0_attn_ref(h, L0_attn_Wq, L0_attn_bq, L0_attn_Wk, L0_attn_bk, L0_attn_Wv, L0_attn_bv, L0_attn_Wo, L0_attn_bo, L0_attn_ln_g, L0_attn_ln_b)
    h = _layernorm(x, axis=-1) * (1 + cb) + sb
    x = x + gb * _L0_ffn_ref(h, L0_ffn_router_w, L0_ffn_w_in, L0_ffn_b_in, L0_ffn_w_out, L0_ffn_b_out)
    return x

_drawn_inputs = setup_inputs


def setup_inputs(seed=0):
    import zlib

    import numpy as np

    out = dict(_drawn_inputs(seed))
    spreads = {'L0_attn_ln_g': (1.0, 0.2),
     'L0_attn_ln_b': (0.0, 0.466),
     'L0_ffn_b_in': (0.0, 0.8),
     'L0_ffn_b_out': (0.0, 0.723)}
    factors = {'L0_attn_Wq': 3.272, 'L0_attn_bq': 32.857, 'L0_attn_bk': 64.0, 'L0_attn_bo': 4.05}
    for name, (base, spread) in spreads.items():
        noise = np.random.default_rng([zlib.crc32(name.encode()), seed]).standard_normal(out[name].shape)
        drawn = base * np.exp(spread * noise) if base else spread * noise
        out[name] = jnp.asarray(drawn.astype(out[name].dtype))
    for name, factor in factors.items():
        out[name] = (out[name] * factor).astype(out[name].dtype)
    return out
```

```python
from contextlib import ExitStack

import concourse.bass as bass
from concourse import mybir

F32 = mybir.dt.float32
F32R = mybir.dt.float32r
ALU = mybir.AluOpType
ACT = mybir.ActivationFunctionType
AX = mybir.AxisListType

P = 128
LN_EPS = 1e-5
GATE_MIN = 0.25
HEAD_DIM = 8
DMA = 16


def adaln_block(nc, x, Wq, bq, Wk, bk, Wv, bv, Wo, bo, ln_g, ln_b, router_w, w_in, b_in, w_out, b_out, c, wmod, out, gate_scratch):
    NB, NTOK, C = x.shape
    T = NTOK // P
    NE = router_w.shape[1]
    HEADS = C // HEAD_DIM
    NMOD = wmod.shape[1] // C
    assert C == P and NTOK == 512 and NE == 8 and w_in.shape[2] == P and NMOD == 6

    x_v = x.rearrange("b (p t) c -> b p (t c)", t=T)
    out_v = out.rearrange("b (p t) c -> b p (t c)", t=T)

    with ExitStack() as ctx:
        def sb(name, shape, dt=F32):
            return ctx.enter_context(nc.sbuf_tensor(name, shape, dt))

        def sem(name):
            return ctx.enter_context(nc.semaphore(name))

        ident = sb("ident", [P, P])
        ones_col = sb("ones_col", [P, 1])
        neg_half = sb("neg_half", [P, T])
        blockmask = sb("blockmask", [P, P])
        w_nat = sb("w_nat", [P, 4, P])
        wqv_hi = sb("wqv_hi", [P, 2, P], F32R)
        wqv_lo = sb("wqv_lo", [P, 2, P], F32R)
        wk_hi = sb("wk_hi", [P, P], F32R)
        wk_lo = sb("wk_lo", [P, P], F32R)
        woT = sb("woT", [P, P])
        wo_gain = sb("wo_gain", [P, P])
        NROW = NE + 3
        rows = sb("rows", [NROW, P])
        cols = sb("cols", [P, NROW])
        bo_bc = sb("bo_bc", [NB, P])
        bv_mask = sb("bv_mask", [P, P])
        bq_ld = sb("bq_ld", [33, P])
        bq_tmp = sb("bq_tmp", [33, P], F32R)
        bq_pad = sb("bq_pad", [P, P], F32R)
        bq_ones = sb("bq_ones", [P, P], F32R)
        bq_ones32 = sb("bq_ones32", [P, P])
        rw = sb("rw", [P, NE])
        win = sb("win", [P, NE, P])
        win_hi = sb("win_hi", [P, NE, P], F32R)
        win_lo = sb("win_lo", [P, NE, P], F32R)
        wout = sb("wout", [P, NE, P])
        bout_ld = sb("bout_ld", [2 * NE, P])
        bout_hi = sb("bout_hi", [P, P], F32R)
        bout_lo = sb("bout_lo", [P, P], F32R)
        sel32 = sb("sel32", [P, NE, P])
        sel = sb("sel", [P, NE, P], F32R)
        c_sb = sb("c_sb", [NB, P])
        silu_c = sb("silu_c", [NB, P])
        silu_cT = sb("silu_cT", [P, NB])
        wmod_sb = sb("wmod_sb", [P, NMOD, P])
        modT = sb("modT", [P, NB, 5])
        gsign_b = sb("gsign_b", [P, NB])
        gabs_b = sb("gabs_b", [P, NB])
        gsign_a = sb("gsign_a", [NB, P])
        gabs_a = sb("gabs_a", [NB, P])
        ga_rows = sb("ga_rows", [NB, 2, P])
        lnb_bc = sb("lnb_bc", [P, NB])
        attn_const = sb("attn_const", [NB, P])
        gates = sb("gates", [P, NB, 2, P])

        x_all = sb("x_all", [P, NB, T, P])
        st1 = sb("st1", [P, T, 6])
        mv1 = sb("mv1", [P, T, 2])
        ve1 = sb("ve1", [P, T])
        rstd1 = sb("rstd1", [P, T])
        xn1 = sb("xn1", [P, T, P])
        modA = sb("modA", [P, 2])
        h = sb("h", [P, NTOK])
        h_hi = sb("h_hi", [P, NTOK], F32R)
        h_lo = sb("h_lo", [P, NTOK], F32R)
        kmax = sb("kmax", [P, 1])
        kbmax = sb("kbmax", [P, 1])
        kshift = sb("kshift", [P, 1])
        ekT = sb("ekT", [P, NTOK])
        ksum = sb("ksum", [P, 1])
        kinv = sb("kinv", [P, 1])
        ek = sb("ek", [P, T, P])
        qmax = sb("qmax", [P, T * HEADS])
        qs = sb("qs", [P, T * HEADS, HEAD_DIM])
        eq = sb("eq", [P, T * HEADS, HEAD_DIM])
        qsum = sb("qsum", [P, T * HEADS])
        qinv = sb("qinv", [P, T * HEADS])
        qn = sb("qn", [P, T * HEADS, HEAD_DIM])
        qT = sb("qT", [P, NTOK])
        v_sb = sb("v_sb", [P, T, P])
        s1 = sb("s1", [P, P])
        s2 = sb("s2", [P, P])
        srow = sb("srow", [P, 1])
        smean = sb("smean", [P, 1])
        s3 = sb("s3", [P, P])
        outT = sb("outT", [P, NTOK])
        sq = sb("sq", [P, NTOK])
        wog = sb("wog", [P, P])
        ve_o = sb("ve_o", [P, T])
        rstd_o = sb("rstd_o", [P, T])
        st2 = sb("st2", [P, T, 6])
        mv2 = sb("mv2", [P, T, 2])
        ve2 = sb("ve2", [P, T])
        rstd2 = sb("rstd2", [P, T])
        xn2 = sb("xn2", [P, T, P])
        modB = sb("modB", [P, 2, 3])
        h2 = sb("h2", [P, NTOK])
        h2_hi = sb("h2_hi", [P, 2, NTOK], F32R)
        h2_lo = sb("h2_lo", [P, 2, NTOK], F32R)
        lg = sb("lg", [P, T, NE])
        top = sb("top", [P, T, 8])
        top2 = sb("top2", [P, T, 8])
        lg_cut = sb("lg_cut", [P, T, NE])
        lshift = sb("lshift", [P, T, NE])
        elg = sb("elg", [P, T, NE])
        esum = sb("esum", [P, T])
        einv = sb("einv", [P, T])
        chosen = sb("chosen", [P, T, NE])
        echosen = sb("echosen", [P, T, NE])
        gate = sb("gate", [P, T, NE])
        gate_hi = sb("gate_hi", [P, T, NE], F32R)
        gate2 = sb("gate2", [P, T, P])
        gateT = sb("gateT", [P, 2, NTOK], F32R)
        u = sb("u", [P, 2, NTOK])
        v = sb("v", [P, 2, NTOK])
        yg = sb("yg", [P, NTOK])

        pH = ctx.enter_context(nc.psum_tensor("pH", [P, 2, NTOK], F32))
        pG = ctx.enter_context(nc.psum_tensor("pG", [P, NTOK], F32))
        pY = ctx.enter_context(nc.psum_tensor("pY", [P, NTOK], F32))
        pB = ctx.enter_context(nc.psum_tensor("pB", [P, NTOK], F32))
        pQV = ctx.enter_context(nc.psum_tensor("pQV", [P, T, 2, P], F32))
        pA = ctx.enter_context(nc.psum_tensor("pA", [P, NTOK], F32))
        pQV_flat = pQV[:, :, :, :].rearrange("p t w c -> p (t w c)")
        pQT = pQV_flat[:, 0:NTOK]
        pS = pQV_flat[:, NTOK:NTOK + P]
        pSSQ = pQV_flat[:, NTOK + P:NTOK + P + T]
        q_view = pQV[:, :, 0, :].rearrange("p t (h d) -> p t h d", d=HEAD_DIM)

        s = {n: sem(n) for n in (
            "x_loaded loads_a loads_b const_set const_ready silu_ready tr_w tr_small cols_ready w_hi_ready prep_w mm_mod prep_mod "
            "mm_const rows_ready gates_stored gates_loaded prep_v prep_b prep_c sel_ready "
            "st1_done mv1_done ve1_done rstd1_ready xn1_ready "
            "hT_done modA_ready h_ready hhi_ready hlo_ready kT_done kmax_done kbmax_done kshift_ready ek_exp kinv_ready qv_done qmax_done qs_ready v_ready "
            "eq_ready qsum_done qinv_ready qn_ready ekT_done ek_ready qT_done qT_ready state_done s1_done s2_done smean_done s_ready out_done "
            "outT_ready sq_ready ssq_done veo_done rstdo_ready xg_ready wog_ready wo_done x1_ready st2_done mv2_done ve2_done rstd2_ready xn2_ready "
            "modB_ready h2T_done h2_ready h2hi_ready h2lo_ready logits_done lg_ready top_done top2_done cut_done lshift_ready elg_ready "
            "esum_done einv_done chosen_done echosen_done gate_done ghi_done gate2_ready gateT_done gateT_ready "
            "mm1_done gelu_done pg_done v_done mm2_done yg_ready yT_done out_ready stored"
        ).split()}

        def w(eng, name, value):
            if not (isinstance(value, int) and value <= 0):
                eng.wait_ge(s[name], value)

        LOADS_A = 12
        LOADS_B = 7
        N_FULL = NB - 3

        def run(eng, step):
            for b in (-3, -2, -1, 0):
                step(b, b % 2)
            with eng.Fori(1, N_FULL - 1, 2) as i:
                step(i, 1)
                step(i + 1, 0)
            for b in range(N_FULL, NB + 1):
                step(b, b % 2)

        def has(b, stage):
            return not isinstance(b, int) or 0 <= b + stage < NB

        block = ctx.enter_context(nc.Block())

        @block.sync
        def _(sp):
            sp.dma_start(x_all[:, 0, :, :], x_v[0]).then_inc(s["x_loaded"], DMA)
            for n in (1, 2):
                sp.wait_ge(s["x_loaded"], DMA * n)
                sp.dma_start(x_all[:, n, :, :], x_v[n]).then_inc(s["x_loaded"], DMA)
            sp.wait_ge(s["rows_ready"], 3)
            sp.dma_start(gate_scratch, ga_rows[:, :, :].rearrange("b w c -> b (w c)")).then_inc(s["gates_stored"], DMA)
            sp.wait_ge(s["gates_stored"], DMA)
            sp.dma_start(gates[:, :, :, :].rearrange("p b w c -> p (b w c)"),
                         gate_scratch.rearrange("(a b) n -> a (b n)", a=1).to_broadcast([P, NB * 2 * P])).then_inc(s["gates_loaded"], DMA)
            with sp.Fori(3, NB) as i:
                sp.wait_ge(s["x_loaded"], DMA * i)
                sp.dma_start(x_all[:, i, :, :], x_v[i]).then_inc(s["x_loaded"], DMA)
            with sp.Fori(0, NB) as i:
                sp.wait_ge(s["out_ready"], i + 1)
                sp.dma_start(out_v[i], x_all[:, i, :, :]).then_inc(s["stored"], DMA)
            sp.wait_ge(s["stored"], DMA * NB)

        @block.gpsimd
        def _(pool):
            pool.memset(ident[:, :], 0.0).then_inc(s["const_set"], 1)
            pool.memset(blockmask[:, :], 1.0).then_inc(s["const_set"], 1)
            pool.memset(sel32[:, :, :], 0.0).then_inc(s["const_set"], 1)
            pool.memset(neg_half[:, :], -0.5)
            pool.memset(ones_col[:, :], 1.0)
            pool.memset(gate2[:, :, :], 0.0)
            pool.memset(top2[:, :, :], 3.0e38).then_inc(s["const_set"], 1)
            pool.wait_ge(s["const_set"], 1)
            pool.affine_select(out=ident[:, :], in_=ident[:, :], compare_op=ALU.not_equal, fill=1.0, base=0,
                               pattern=[[-1, P]], channel_multiplier=1).then_inc(s["const_ready"], 1)
            pool.wait_ge(s["const_set"], 2)
            bm = blockmask[:, :].rearrange("p (h d) -> p h d", d=HEAD_DIM)
            pool.affine_select(out=bm, in_=bm, compare_op=ALU.is_ge, fill=0.0, base=0,
                               pattern=[[-HEAD_DIM, HEADS], [0, HEAD_DIM]], channel_multiplier=1).then_inc(s["const_set"], 1)
            pool.wait_ge(s["const_set"], 5)
            pool.affine_select(out=bm, in_=bm, compare_op=ALU.is_ge, fill=0.0, base=HEAD_DIM - 1,
                               pattern=[[HEAD_DIM, HEADS], [0, HEAD_DIM]], channel_multiplier=-1).then_inc(s["const_ready"], 1)
            pool.affine_select(out=sel32[:, :, :], in_=sel32[:, :, :], compare_op=ALU.not_equal, fill=1.0, base=0,
                               pattern=[[-1, NE], [0, P]], channel_multiplier=1).then_inc(s["const_set"], 1)
            pool.wait_ge(s["const_set"], 6)
            pool.affine_select(out=sel32[:, :, :], in_=sel32[:, :, :], compare_op=ALU.not_equal, fill=1.0, base=-NE,
                               pattern=[[-1, NE], [0, P]], channel_multiplier=1).then_inc(s["const_ready"], 1)

            def rstd_L(n):
                pool.wait_ge(s["ve1_done"], n + 1)
                pool.tensor_tensor(rstd1[:, :], ve1[:, :], neg_half[:, :], ALU.pow).then_inc(s["rstd1_ready"], 1)

            def mod_A(n):
                pool.tensor_copy(modA[:, :], modT[:, n, 0:2]).then_inc(s["modA_ready"], 1)

            def mod_B(n, par):
                pool.tensor_copy(modB[:, par, :], modT[:, n, 2:5]).then_inc(s["modB_ready"], 1)

            def gated_const(n):
                pool.tensor_tensor(x_all[:, n, :, :], x_all[:, n, :, :],
                                   gates[:, n, 1, :].unsqueeze(1).to_broadcast([P, T, P]), ALU.add).then_inc(s["xg_ready"], 1)
                pool.tensor_tensor(wog[:, :], wo_gain[:, :], gates[:, n, 0, :], ALU.mult).then_inc(s["wog_ready"], 1)

            def q_norm(n):
                pool.wait_ge(s["qinv_ready"], n + 1)
                pool.tensor_tensor(qn[:, :, :], eq[:, :, :], qinv[:, :].unsqueeze(2).to_broadcast([P, T * HEADS, HEAD_DIM]),
                                   ALU.mult).then_inc(s["qn_ready"], 1)

            def rstd_O(n):
                pool.wait_ge(s["veo_done"], n + 1)
                pool.tensor_tensor(rstd_o[:, :], ve_o[:, :], neg_half[:, :], ALU.pow).then_inc(s["rstdo_ready"], 1)

            def rstd_B(n):
                pool.wait_ge(s["ve2_done"], n + 1)
                pool.tensor_tensor(rstd2[:, :], ve2[:, :], neg_half[:, :], ALU.pow).then_inc(s["rstd2_ready"], 1)

            def step(b, par):
                if isinstance(b, int) and b == -2:
                    pool.wait_ge(s["prep_mod"], 5)
                    pool.wait_ge(s["gates_loaded"], DMA)
                    pool.wait_ge(s["prep_c"], 1)
                if has(b, 1) and has(b, 1):
                    w(pool, "out_ready", b)
                    mod_B(b + 1, (par + 1) % 2)
                if has(b, 2):
                    w(pool, "hhi_ready", b + 2)
                    mod_A(b + 2)
                    pool.wait_ge(s["xn1_ready"], T * (b + 3))
                    w(pool, "wo_done", b + 2)
                    gated_const(b + 2)
                    q_norm(b + 2)
                if has(b, 3):
                    rstd_L(b + 3)
                if has(b, 2):
                    rstd_O(b + 2)
                    rstd_B(b + 2)
            run(pool, step)

        @block.scalar
        def _(act):
            la, lb = s["loads_a"], s["loads_b"]
            act.dma_start(c_sb[:, :], c).then_inc(la, DMA)
            act.dma_start(wmod_sb[:, :, :], wmod.rearrange("k (j c) -> k j c", j=NMOD)).then_inc(la, DMA)
            for j, wt in enumerate((Wq, Wv, Wk, Wo)):
                act.dma_start(w_nat[:, j, :], wt).then_inc(la, DMA)
            act.dma_start(rows[0:NE, :], b_in).then_inc(la, DMA)
            for j, r in enumerate((bk, ln_g, ln_b)):
                act.dma_start(rows[NE + j:NE + j + 1, :], r.rearrange("(a n) -> a n", a=1)).then_inc(la, DMA)
            act.dma_start(bo_bc[:, :], bo.rearrange("(a n) -> a n", a=1).to_broadcast([NB, P])).then_inc(la, DMA)
            act.dma_start(bv_mask[:, :], bv.rearrange("(a n) -> a n", a=1).to_broadcast([P, P])).then_inc(la, DMA)
            act.dma_start(bq_ld[0:1, :], bq.rearrange("(a n) -> a n", a=1)).then_inc(lb, DMA)
            act.dma_start(bq_ld[32:33, :], bq.rearrange("(a n) -> a n", a=1)).then_inc(lb, DMA)
            act.dma_start(rw[:, :], router_w).then_inc(lb, DMA)
            act.dma_start(win[:, :, :], w_in.rearrange("e d h -> d e h")).then_inc(lb, DMA)
            act.dma_start(wout[:, :, :], w_out.rearrange("e h d -> h e d")).then_inc(lb, DMA)
            act.dma_start(bout_ld[0:NE, :], b_out).then_inc(lb, DMA)
            act.dma_start(bout_ld[NE:2 * NE, :], b_out).then_inc(lb, DMA)
            act.wait_ge(la, DMA * LOADS_A)
            act.activation(silu_c[:, :], c_sb[:, :], ACT.Silu).then_inc(s["silu_ready"], 1)
            act.wait_ge(s["tr_w"], 4)
            act.activation(wqv_hi[:, :, :].rearrange("p a c -> p (a c)"), pQT[:, 0:2 * P], ACT.Copy).then_inc(s["w_hi_ready"], 1)
            act.activation(wk_hi[:, :], pQT[:, 2 * P:3 * P], ACT.Copy).then_inc(s["w_hi_ready"], 1)
            act.activation(woT[:, :], pQT[:, 3 * P:4 * P], ACT.Copy).then_inc(s["w_hi_ready"], 1)
            act.wait_ge(lb, DMA * LOADS_B)
            act.activation(win_hi[:, :, :], win[:, :, :], ACT.Copy).then_inc(s["w_hi_ready"], 1)

            def h_evac(n):
                act.wait_ge(s["hT_done"], n + 1)
                act.wait_ge(s["modA_ready"], n + 1)
                act.activation(h[:, :], pA[:, :], ACT.Identity, bias=modA[:, 1:2], scale=modA[:, 0:1]).then_inc(s["h_ready"], 1)
                act.activation(h_hi[:, :], pA[:, :], ACT.Identity, bias=modA[:, 1:2], scale=modA[:, 0:1]).then_inc(s["hhi_ready"], 1)

            def h2_evac(n, par):
                act.wait_ge(s["h2T_done"], n + 1)
                act.wait_ge(s["modB_ready"], n + 1)
                act.activation(h2[:, :], pB[:, :], ACT.Identity, bias=modB[:, par, 1:2], scale=modB[:, par, 0:1]).then_inc(s["h2_ready"], 1)
                act.activation(h2_hi[:, par, :], pB[:, :], ACT.Identity, bias=modB[:, par, 1:2], scale=modB[:, par, 0:1]).then_inc(s["h2hi_ready"], 1)

            def exp_k(n):
                act.wait_ge(s["kshift_ready"], n + 1)
                act.activation(ekT[:, :], pA[:, :], ACT.Exp, bias=kshift[:, 0:1], accum_out=ksum[:, :]).then_inc(s["ek_exp"], 1)

            def exp_q(n):
                act.wait_ge(s["qs_ready"], n + 1)
                act.activation(eq[:, :, :], qs[:, :, :], ACT.Exp).then_inc(s["eq_ready"], 1)

            def exp_router(n):
                act.wait_ge(s["lshift_ready"], n + 1)
                act.activation(elg[:, :, :], lshift[:, :, :], ACT.Exp).then_inc(s["elg_ready"], 1)

            def ek_evac(n):
                act.wait_ge(s["ekT_done"], n + 1)
                act.activation(ek[:, :, :].rearrange("p t c -> p (t c)"), pA[:, :], ACT.Copy).then_inc(s["ek_ready"], 1)

            def qT_evac(n):
                act.wait_ge(s["qT_done"], n + 1)
                act.activation(qT[:, :], pQT, ACT.Copy).then_inc(s["qT_ready"], 1)

            def outT_evac(n):
                act.wait_ge(s["out_done"], n + 1)
                act.activation(sq[:, :], pA[:, :], ACT.Square).then_inc(s["sq_ready"], 1)
                act.activation(outT[:, :], pA[:, :], ACT.Copy).then_inc(s["outT_ready"], 1)

            def gateT_evac(n, par):
                act.wait_ge(s["gateT_done"], n + 1)
                act.activation(gateT[:, par, :], pB[:, :], ACT.Copy).then_inc(s["gateT_ready"], 1)

            def gelu(b, e):
                act.wait_ge(s["mm1_done"], NE * b + e + 1)
                w(act, "v_done", NE * b + e - 1)
                act.activation(u[:, e % 2, :], pH[:, e % 2, :], ACT.Gelu_apprx_tanh, bias=cols[:, e:e + 1]).then_inc(s["gelu_done"], 1)

            def y_gate(b, par):
                act.wait_ge(s["mm2_done"], NE * (b + 1))
                act.activation(yg[:, :], pY[:, :], ACT.Copy, scale=modB[:, par, 2:3]).then_inc(s["yg_ready"], 1)

            def step(b, par):
                M, B, A = has(b, 0), has(b, 1), has(b, 2)
                if has(b, -1):
                    y_gate(b - 1, (par + 1) % 2)
                if M:
                    gelu(b, 0)
                if A:
                    h_evac(b + 2)
                if M:
                    gelu(b, 1)
                if B:
                    h2_evac(b + 1, (par + 1) % 2)
                if M:
                    gelu(b, 2)
                    gelu(b, 3)
                if A:
                    exp_k(b + 2)
                    exp_q(b + 2)
                if B:
                    exp_router(b + 1)
                if A:
                    ek_evac(b + 2)
                if M:
                    gelu(b, 4)
                if A:
                    qT_evac(b + 2)
                if M:
                    gelu(b, 5)
                if B:
                    gateT_evac(b + 1, (par + 1) % 2)
                if A:
                    outT_evac(b + 2)
                if M:
                    gelu(b, 6)
                    gelu(b, 7)
            run(act, step)

        @block.tensor
        def _(pe):
            mm = pe.matmul
            pe.wait_ge(s["const_ready"], 1)
            pe.wait_ge(s["loads_a"], DMA * LOADS_A)
            for j in range(4):
                pe.transpose(pQT[:, j * P:(j + 1) * P], w_nat[:, j, :], ident[:, :]).then_inc(s["tr_w"], 1)
            pe.transpose(pA[:, 0:NROW], rows[:, :], ident[0:NROW, 0:NROW]).then_inc(s["tr_small"], 1)
            pe.wait_ge(s["silu_ready"], 1)
            pe.transpose(pH[:, 0, 0:NB], silu_c[:, :], ident[0:NB, 0:NB]).then_inc(s["tr_small"], 1)
            pe.wait_ge(s["cols_ready"], 3)
            for i, j in enumerate((1, 0, 4, 3, 5)):
                mm(pB[:, i * NB:(i + 1) * NB], wmod_sb[:, j, :], silu_cT[:, :], start=True, stop=True)
            mm(pY[0:NB, 0:P], silu_cT[:, :], wmod_sb[:, 2, :], start=True, stop=True)
            pe.wait_ge(s["w_hi_ready"], 3)
            mm(pY[0:NB, P:2 * P], lnb_bc[:, :], woT[:, :], start=True, stop=True).then_inc(s["mm_mod"], 1)
            pe.wait_ge(s["prep_w"], 8)

            def hT(n):
                pe.wait_ge(s["xn1_ready"], T * (n + 1))
                w(pe, "outT_ready", n)
                for t in range(T):
                    i = pe.transpose(pA[:, t * P:(t + 1) * P], xn1[:, t, :], ident[:, :])
                i.then_inc(s["hT_done"], 1)

            def kT(n):
                pe.wait_ge(s["hlo_ready"], n + 1)
                mm(pA[:, :], wk_hi[:, :], h_hi[:, :], start=True, stop=False)
                mm(pA[:, :], wk_lo[:, :], h_hi[:, :], start=False, stop=False)
                mm(pA[:, :], wk_hi[:, :], h_lo[:, :], start=False, stop=True).then_inc(s["kT_done"], 1)

            def qv(n):
                w(pe, "x1_ready", T * n)
                hi = wqv_hi[:, :, :].rearrange("p a c -> p (a c)")
                lo = wqv_lo[:, :, :].rearrange("p a c -> p (a c)")
                for t in range(T):
                    o = pQV[:, t, :, :].rearrange("p a c -> p (a c)")
                    ts = slice(t * P, (t + 1) * P)
                    mm(o, h_hi[:, ts], hi, start=True, stop=False)
                    mm(o, h_hi[:, ts], lo, start=False, stop=False)
                    mm(pQV[:, t, 0, :], bq_ones[:, :], bq_pad[:, :], start=False, stop=False)
                    i = mm(o, h_lo[:, ts], hi, start=False, stop=True)
                i.then_inc(s["qv_done"], 1)

            def ek_back(n):
                pe.wait_ge(s["ek_exp"], n + 1)
                for t in range(T):
                    i = pe.transpose(pA[:, t * P:(t + 1) * P], ekT[:, t * P:(t + 1) * P], ident[:, :])
                i.then_inc(s["ekT_done"], 1)

            def q_turn(n):
                pe.wait_ge(s["v_ready"], n + 1)
                pe.wait_ge(s["qn_ready"], n + 1)
                qf = qn[:, :, :].rearrange("p a d -> p (a d)")
                for t in range(T):
                    i = pe.transpose(pQT[:, t * P:(t + 1) * P], qf[:, t * P:(t + 1) * P], ident[:, :])
                i.then_inc(s["qT_done"], 1)

            def state(n):
                pe.wait_ge(s["v_ready"], n + 1)
                pe.wait_ge(s["ek_ready"], n + 1)
                for t in range(T):
                    i = mm(pS, ek[:, t, :], v_sb[:, t, :], start=(t == 0), stop=(t == T - 1))
                i.then_inc(s["state_done"], 1)

            def attend(n):
                pe.wait_ge(s["s_ready"], n + 1)
                pe.wait_ge(s["qT_ready"], n + 1)
                mm(pA[:, :], s3[:, :], qT[:, :], start=True, stop=True).then_inc(s["out_done"], 1)

            def ssq(n):
                pe.wait_ge(s["sq_ready"], n + 1)
                for t in range(T):
                    i = mm(pSSQ[:, t:t + 1], sq[:, t * P:(t + 1) * P], ones_col[:, :], start=True, stop=True)
                i.then_inc(s["ssq_done"], 1)

            def project(n):
                pe.wait_ge(s["outT_ready"], n + 1)
                pe.wait_ge(s["wog_ready"], n + 1)
                for t in range(T):
                    i = mm(pQT[:, t * P:(t + 1) * P], outT[:, t * P:(t + 1) * P], wog[:, :], start=True, stop=True)
                i.then_inc(s["wo_done"], 1)

            def h2T(n):
                pe.wait_ge(s["xn2_ready"], T * (n + 1))
                w(pe, "out_ready", n - 1)
                w(pe, "gateT_ready", n)
                for t in range(T):
                    i = pe.transpose(pB[:, t * P:(t + 1) * P], xn2[:, t, :], ident[:, :])
                i.then_inc(s["h2T_done"], 1)

            def logits(n):
                pe.wait_ge(s["h2hi_ready"], n + 1)
                for t in range(T):
                    i = mm(pB[:, t * NE:(t + 1) * NE], h2[:, t * P:(t + 1) * P], rw[:, :], start=True, stop=True)
                i.then_inc(s["logits_done"], 1)

            def gate_turn(n):
                pe.wait_ge(s["gate2_ready"], n + 1)
                for t in range(T):
                    i = pe.transpose(pB[:, t * P:(t + 1) * P], gate2[:, t, :], ident[:, :])
                i.then_inc(s["gateT_done"], 1)

            def hidden(b, par, e):
                if e == 0:
                    pe.wait_ge(s["h2lo_ready"], b + 1)
                w(pe, "gelu_done", NE * b + e - 1)
                o = pH[:, e % 2, :]
                mm(o, win_hi[:, e, :], h2_hi[:, par, :], start=True, stop=False)
                mm(o, win_lo[:, e, :], h2_hi[:, par, :], start=False, stop=False)
                mm(o, win_hi[:, e, :], h2_lo[:, par, :], start=False, stop=True).then_inc(s["mm1_done"], 1)

            def spread_gate(b, par, e):
                if e == 0:
                    pe.wait_ge(s["gateT_ready"], b + 1)
                w(pe, "v_done", NE * b + e)
                mm(pG[:, :], sel[:, e, :], gateT[:, par, :], start=True, stop=True).then_inc(s["pg_done"], 1)

            def combine(b, par, e):
                if e == 0:
                    w(pe, "yg_ready", b)
                    mm(pY[:, :], bout_hi[:, :], gateT[:, par, :], start=True, stop=False)
                    mm(pY[:, :], bout_lo[:, :], gateT[:, par, :], start=False, stop=False)
                pe.wait_ge(s["v_done"], NE * b + e + 1)
                mm(pY[:, :], wout[:, e, :], v[:, e % 2, :], start=False, stop=(e == NE - 1)).then_inc(s["mm2_done"], 1)

            def y_turn(b):
                pe.wait_ge(s["yg_ready"], b + 1)
                w(pe, "gateT_ready", b + 2 if not isinstance(b, int) else min(b + 2, NB))
                for t in range(T):
                    i = pe.transpose(pB[:, t * P:(t + 1) * P], yg[:, t * P:(t + 1) * P], ident[:, :])
                i.then_inc(s["yT_done"], 1)

            def step(b, par):
                M, B, A = has(b, 0), has(b, 1), has(b, 2)
                nxt = (par + 1) % 2
                if M:
                    hidden(b, par, 0)
                    spread_gate(b, par, 0)
                if A:
                    hT(b + 2)
                if has(b, -1):
                    y_turn(b - 1)
                if M:
                    hidden(b, par, 1)
                    combine(b, par, 0)
                    spread_gate(b, par, 1)
                if A:
                    kT(b + 2)
                if B:
                    h2T(b + 1)
                if M:
                    hidden(b, par, 2)
                    combine(b, par, 1)
                    spread_gate(b, par, 2)
                if A:
                    qv(b + 2)
                if B:
                    logits(b + 1)
                if M:
                    hidden(b, par, 3)
                    combine(b, par, 2)
                    spread_gate(b, par, 3)
                    hidden(b, par, 4)
                    combine(b, par, 3)
                    spread_gate(b, par, 4)
                if A:
                    ek_back(b + 2)
                    state(b + 2)
                if M:
                    hidden(b, par, 5)
                    combine(b, par, 4)
                    spread_gate(b, par, 5)
                if A:
                    q_turn(b + 2)
                if B:
                    gate_turn(b + 1)
                if A:
                    attend(b + 2)
                if M:
                    hidden(b, par, 6)
                    combine(b, par, 5)
                    spread_gate(b, par, 6)
                if A:
                    ssq(b + 2)
                    project(b + 2)
                if M:
                    hidden(b, par, 7)
                    combine(b, par, 6)
                    spread_gate(b, par, 7)
                    combine(b, par, 7)
            run(pe, step)

        @block.vector
        def _(dve):
            dve.memset(bq_pad[:, :].bitcast(F32), 0.0)
            dve.memset(bq_ones32[:, :], 0.0)
            dve.memset(bout_hi[:, :].bitcast(F32), 0.0)
            dve.memset(bout_lo[:, :].bitcast(F32), 0.0).then_inc(s["prep_v"], 1)
            dve.wait_ge(s["prep_v"], 1)
            dve.memset(bq_ones32[0:1, :], 1.0)
            dve.memset(bq_ones32[32:33, :], 1.0).then_inc(s["prep_v"], 1)
            dve.wait_ge(s["prep_v"], 2)
            dve.tensor_copy(bq_ones[:, :], bq_ones32[:, :]).then_inc(s["prep_w"], 1)
            dve.wait_ge(s["tr_small"], 1)
            dve.tensor_copy(cols[:, :], pA[:, 0:NROW]).then_inc(s["cols_ready"], 1)
            dve.wait_ge(s["cols_ready"], 1)
            dve.tensor_copy(lnb_bc[:, :], cols[:, NE + 2:NE + 3].to_broadcast([P, NB])).then_inc(s["cols_ready"], 1)
            dve.wait_ge(s["tr_small"], 2)
            dve.tensor_copy(silu_cT[:, :], pH[:, 0, 0:NB]).then_inc(s["cols_ready"], 1)
            dve.wait_ge(s["w_hi_ready"], 3)
            dve.tensor_tensor(wqv_lo[:, :, :].rearrange("p a c -> p (a c)"), pQT[:, 0:2 * P],
                              wqv_hi[:, :, :].rearrange("p a c -> p (a c)").bitcast(F32), ALU.subtract).then_inc(s["prep_w"], 1)
            dve.tensor_tensor(wk_lo[:, :], pQT[:, 2 * P:3 * P], wk_hi[:, :].bitcast(F32), ALU.subtract).then_inc(s["prep_w"], 1)
            dve.tensor_scalar(wo_gain[:, :], woT[:, :], cols[:, NE + 1:NE + 2], None, ALU.mult).then_inc(s["prep_c"], 1)
            dve.wait_ge(s["mm_mod"], 1)
            pmod = pB[:, 0:5 * NB].rearrange("p (i b) -> p i b", b=NB)
            for i, plus in enumerate((1.0, 0.0, 1.0, 0.0)):
                dve.tensor_scalar(modT[:, :, i], pmod[:, i, :], plus, None, ALU.add).then_inc(s["prep_mod"], 1)

            def hold_gate(sign, mag, src, dst, done):
                dve.tensor_scalar(sign, src, 0.0, 2.0, ALU.is_ge, ALU.mult)
                dve.tensor_copy(mag, src).then_inc(s["prep_v"], 1)
                hold_gate.count += 1
                dve.wait_ge(s["prep_v"], hold_gate.count)
                dve.scalar_tensor_tensor(out=mag, in0=mag, scalar=-1.0, in1=src, op0=ALU.mult, op1=ALU.max).then_inc(s["prep_v"], 1)
                hold_gate.count += 1
                dve.wait_ge(s["prep_v"], hold_gate.count)
                dve.tensor_scalar(mag, mag, GATE_MIN, None, ALU.max).then_inc(s["prep_v"], 1)
                hold_gate.count += 1
                dve.wait_ge(s["prep_v"], hold_gate.count)
                dve.scalar_tensor_tensor(out=dst, in0=sign, scalar=-1.0, in1=mag, op0=ALU.add, op1=ALU.mult).then_inc(s[done], 1)
            hold_gate.count = 2
            hold_gate(gsign_b[:, :], gabs_b[:, :], pmod[:, 4, :], modT[:, :, 4], "prep_mod")
            hold_gate(gsign_a[:, :], gabs_a[:, :], pY[0:NB, 0:P], ga_rows[:, 0, :], "rows_ready")
            dve.tensor_tensor(attn_const[:, :], pY[0:NB, P:2 * P], bo_bc[:, :], ALU.add).then_inc(s["rows_ready"], 1)
            dve.wait_ge(s["rows_ready"], 2)
            dve.tensor_tensor(ga_rows[:, 1, :], ga_rows[:, 0, :], attn_const[:, :], ALU.mult).then_inc(s["rows_ready"], 1)
            dve.wait_ge(s["const_ready"], 3)
            dve.wait_ge(s["loads_a"], DMA * LOADS_A)
            dve.tensor_tensor(bv_mask[:, :], bv_mask[:, :], blockmask[:, :], ALU.mult).then_inc(s["prep_b"], 1)
            dve.tensor_copy(sel[:, :, :], sel32[:, :, :]).then_inc(s["prep_w"], 1)
            dve.wait_ge(s["loads_b"], DMA * LOADS_B)
            dve.tensor_copy(bq_pad[0:1, :], bq_ld[0:1, :]).then_inc(s["prep_w"], 1)
            dve.tensor_copy(bq_tmp[32:33, :], bq_ld[32:33, :])
            dve.tensor_copy(bout_hi[0:2 * NE, :], bout_ld[:, :]).then_inc(s["prep_v"], 1)
            dve.wait_ge(s["prep_v"], hold_gate.count + 1)
            dve.tensor_tensor(bq_pad[32:33, :], bq_ld[32:33, :], bq_tmp[32:33, :].bitcast(F32), ALU.subtract).then_inc(s["prep_w"], 1)
            dve.tensor_tensor(bout_lo[0:2 * NE, :], bout_ld[:, :], bout_hi[0:2 * NE, :].bitcast(F32), ALU.subtract).then_inc(s["prep_w"], 1)
            dve.wait_ge(s["w_hi_ready"], 4)
            dve.tensor_tensor(win_lo[:, :, :], win[:, :, :], win_hi[:, :, :].bitcast(F32), ALU.subtract).then_inc(s["prep_w"], 1)
            dve.wait_ge(s["prep_b"], 1)

            def x_here(n):
                dve.wait_ge(s["x_loaded"], DMA * (n + 1))

            def ln1_stats(n):
                for t in range(T):
                    dve.bn_stats(st1[:, t, :], x_all[:, n, t, :]).then_inc(s["st1_done"], 1)

            def ln1_stats_here(n):
                dve.wait_ge(s["st1_done"], T * n + T)

            def ln1_var(n):
                for t in range(T):
                    dve.bn_aggr(mv1[:, t, :], st1[:, t, :]).then_inc(s["mv1_done"], 1)
                dve.wait_ge(s["mv1_done"], T * n + T)
                dve.tensor_scalar(ve1[:, :], mv1[:, :, 1], LN_EPS, None, ALU.add).then_inc(s["ve1_done"], 1)

            def ln1_apply(n):
                dve.wait_ge(s["rstd1_ready"], n + 1)
                w(dve, "hT_done", n)
                for t in range(T):
                    dve.tensor_scalar(xn1[:, t, :], x_all[:, n, t, :], mv1[:, t, 0:1], rstd1[:, t:t + 1],
                                      ALU.subtract, ALU.mult).then_inc(s["xn1_ready"], 1)

            def h_low(n):
                dve.wait_ge(s["hhi_ready"], n + 1)
                dve.tensor_tensor(h_lo[:, :], h[:, :], h_hi[:, :].bitcast(F32), ALU.subtract).then_inc(s["hlo_ready"], 1)

            def k_max(n):
                dve.wait_ge(s["kT_done"], n + 1)
                dve.tensor_reduce(kmax[:, :], pA[:, :], AX.X, ALU.max).then_inc(s["kmax_done"], 1)
                dve.wait_ge(s["kmax_done"], n + 1)
                dve.tensor_tensor(kbmax[:, :], kmax[:, :], cols[:, NE:NE + 1], ALU.add).then_inc(s["kbmax_done"], 1)
                dve.wait_ge(s["kbmax_done"], n + 1)
                dve.tensor_tensor(kshift[:, :], cols[:, NE:NE + 1], kbmax[:, :], ALU.subtract).then_inc(s["kshift_ready"], 1)

            def q_shift(n):
                dve.wait_ge(s["qv_done"], n + 1)
                dve.tensor_reduce(qmax[:, :].rearrange("p (t h) -> p t h", t=T), q_view, AX.X, ALU.max).then_inc(s["qmax_done"], 1)
                dve.tensor_copy(v_sb[:, :, :], pQV[:, :, 1, :]).then_inc(s["v_ready"], 1)
                dve.wait_ge(s["qmax_done"], n + 1)
                dve.tensor_tensor(qs[:, :, :].rearrange("p (t h) d -> p t h d", t=T), q_view,
                                  qmax[:, :].rearrange("p (t h) -> p t h", t=T).unsqueeze(3).to_broadcast([P, T, HEADS, HEAD_DIM]),
                                  ALU.subtract).then_inc(s["qs_ready"], 1)

            def q_sum(n):
                dve.wait_ge(s["eq_ready"], n + 1)
                dve.tensor_reduce(qsum[:, :], eq[:, :, :], AX.X, ALU.add).then_inc(s["qsum_done"], 1)
                dve.wait_ge(s["qsum_done"], n + 1)
                dve.reciprocal(qinv[:, :], qsum[:, :]).then_inc(s["qinv_ready"], 1)

            def k_inv(n):
                dve.wait_ge(s["ek_exp"], n + 1)
                dve.reciprocal(kinv[:, :], ksum[:, :]).then_inc(s["kinv_ready"], 1)

            def state_out(n):
                dve.wait_ge(s["state_done"], n + 1)
                dve.wait_ge(s["kinv_ready"], n + 1)
                dve.scalar_tensor_tensor(out=s1[:, :], in0=pS, scalar=kinv[:, 0:1], in1=blockmask[:, :],
                                         op0=ALU.mult, op1=ALU.mult).then_inc(s["s1_done"], 1)
                dve.wait_ge(s["s1_done"], n + 1)
                dve.scalar_tensor_tensor(out=s2[:, :], in0=s1[:, :], scalar=1.0, in1=bv_mask[:, :], op0=ALU.mult, op1=ALU.add,
                                         accum_out=srow[:, :]).then_inc(s["s2_done"], 1)
                dve.wait_ge(s["s2_done"], n + 1)
                dve.tensor_scalar(smean[:, :], srow[:, :], -1.0 / C, None, ALU.mult).then_inc(s["smean_done"], 1)
                dve.wait_ge(s["smean_done"], n + 1)
                dve.tensor_scalar(s3[:, :], s2[:, :], smean[:, 0:1], None, ALU.add).then_inc(s["s_ready"], 1)

            def out_var(n):
                dve.wait_ge(s["ssq_done"], n + 1)
                dve.tensor_scalar(ve_o[:, :], pSSQ, 1.0 / C, LN_EPS, ALU.mult, ALU.add).then_inc(s["veo_done"], 1)

            def residual1(n):
                dve.wait_ge(s["wo_done"], n + 1)
                dve.wait_ge(s["rstdo_ready"], n + 1)
                dve.wait_ge(s["xg_ready"], n + 1)
                for t in range(T):
                    dve.scalar_tensor_tensor(out=x_all[:, n, t, :], in0=pQT[:, t * P:(t + 1) * P], scalar=rstd_o[:, t:t + 1],
                                             in1=x_all[:, n, t, :], op0=ALU.mult, op1=ALU.add).then_inc(s["x1_ready"], 1)

            def x1_here(n):
                dve.wait_ge(s["x1_ready"], T * n + T)

            def ln2_stats(n):
                for t in range(T):
                    dve.bn_stats(st2[:, t, :], x_all[:, n, t, :]).then_inc(s["st2_done"], 1)

            def ln2_stats_here(n):
                dve.wait_ge(s["st2_done"], T * n + T)

            def ln2_var(n):
                for t in range(T):
                    dve.bn_aggr(mv2[:, t, :], st2[:, t, :]).then_inc(s["mv2_done"], 1)
                dve.wait_ge(s["mv2_done"], T * n + T)
                dve.tensor_scalar(ve2[:, :], mv2[:, :, 1], LN_EPS, None, ALU.add).then_inc(s["ve2_done"], 1)

            def ln2_apply(n):
                dve.wait_ge(s["rstd2_ready"], n + 1)
                w(dve, "h2T_done", n)
                for t in range(T):
                    dve.tensor_scalar(xn2[:, t, :], x_all[:, n, t, :], mv2[:, t, 0:1], rstd2[:, t:t + 1],
                                      ALU.subtract, ALU.mult).then_inc(s["xn2_ready"], 1)

            def h2_low(n, par):
                dve.wait_ge(s["h2hi_ready"], n + 1)
                dve.tensor_tensor(h2_lo[:, par, :], h2[:, :], h2_hi[:, par, :].bitcast(F32), ALU.subtract).then_inc(s["h2lo_ready"], 1)

            def route(n):
                dve.wait_ge(s["logits_done"], n + 1)
                dve.tensor_copy(lg[:, :, :].rearrange("p t e -> p (t e)"), pB[:, 0:T * NE]).then_inc(s["lg_ready"], 1)
                for t in range(T):
                    dve.max(top[:, t, :], pB[:, t * NE:(t + 1) * NE]).then_inc(s["top_done"], 1)
                dve.wait_ge(s["top_done"], T * n + T)
                dve.tensor_copy(top2[:, :, 0:2], top[:, :, 0:2]).then_inc(s["top2_done"], 1)
                dve.wait_ge(s["lg_ready"], n + 1)
                dve.wait_ge(s["top2_done"], n + 1)
                dve.tensor_tensor(lshift[:, :, :], lg[:, :, :], top[:, :, 0:1].to_broadcast([P, T, NE]),
                                  ALU.subtract).then_inc(s["lshift_ready"], 1)
                for t in range(T):
                    dve.match_replace(lg_cut[:, t, :], top2[:, t, :], lg[:, t, :], -3.0e38).then_inc(s["cut_done"], 1)

            def gates_out(n):
                dve.wait_ge(s["cut_done"], T * n + T)
                dve.tensor_tensor(chosen[:, :, :], lg[:, :, :], lg_cut[:, :, :], ALU.not_equal).then_inc(s["chosen_done"], 1)
                dve.wait_ge(s["elg_ready"], n + 1)
                dve.tensor_reduce(esum[:, :], elg[:, :, :], AX.X, ALU.add).then_inc(s["esum_done"], 1)
                dve.wait_ge(s["chosen_done"], n + 1)
                dve.tensor_tensor(echosen[:, :, :], elg[:, :, :], chosen[:, :, :], ALU.mult).then_inc(s["echosen_done"], 1)
                dve.wait_ge(s["esum_done"], n + 1)
                dve.reciprocal(einv[:, :], esum[:, :]).then_inc(s["einv_done"], 1)
                dve.wait_ge(s["einv_done"], n + 1)
                dve.tensor_tensor(gate[:, :, :], echosen[:, :, :], einv[:, :].unsqueeze(2).to_broadcast([P, T, NE]),
                                  ALU.mult).then_inc(s["gate_done"], 1)
                dve.wait_ge(s["gate_done"], n + 1)
                dve.tensor_copy(gate_hi[:, :, :], gate[:, :, :]).then_inc(s["ghi_done"], 1)
                dve.wait_ge(s["ghi_done"], n + 1)
                w(dve, "gateT_done", n)
                dve.tensor_copy(gate2[:, :, 0:NE], gate_hi[:, :, :].bitcast(F32))
                dve.tensor_tensor(gate2[:, :, NE:2 * NE], gate[:, :, :], gate_hi[:, :, :].bitcast(F32),
                                  ALU.subtract).then_inc(s["gate2_ready"], 1)

            def weigh(b, e):
                dve.wait_ge(s["gelu_done"], NE * b + e + 1)
                dve.wait_ge(s["pg_done"], NE * b + e + 1)
                w(dve, "mm2_done", NE * b + e - 1)
                dve.tensor_tensor(v[:, e % 2, :], u[:, e % 2, :], pG[:, :], ALU.mult).then_inc(s["v_done"], 1)

            def residual2(b):
                dve.wait_ge(s["yT_done"], b + 1)
                xb = x_all[:, b, :, :]
                dve.tensor_tensor(xb, pB[:, :].rearrange("p (t c) -> p t c", t=T), xb, ALU.add).then_inc(s["out_ready"], 1)

            def step(b, par):
                M, B, A, L = has(b, 0), has(b, 1), has(b, 2), has(b, 3)
                nxt = (par + 1) % 2
                if M:
                    weigh(b, 0)
                if B:
                    ln2_apply(b + 1)
                if has(b, -1):
                    residual2(b - 1)
                if A:
                    h_low(b + 2)
                if M:
                    weigh(b, 1)
                if B:
                    h2_low(b + 1, nxt)
                if A:
                    k_max(b + 2)
                if L:
                    x_here(b + 3)
                if M:
                    weigh(b, 2)
                if A:
                    q_shift(b + 2)
                if B:
                    route(b + 1)
                if L:
                    ln1_stats(b + 3)
                    ln1_stats_here(b + 3)
                if M:
                    weigh(b, 3)
                if L:
                    ln1_var(b + 3)
                if A:
                    k_inv(b + 2)
                    q_sum(b + 2)
                if M:
                    weigh(b, 4)
                if B:
                    gates_out(b + 1)
                if A:
                    state_out(b + 2)
                if L:
                    ln1_apply(b + 3)
                if M:
                    weigh(b, 5)
                if A:
                    out_var(b + 2)
                    residual1(b + 2)
                    x1_here(b + 2)
                if M:
                    weigh(b, 6)
                if A:
                    ln2_stats(b + 2)
                    ln2_stats_here(b + 2)
                if M:
                    weigh(b, 7)
                if A:
                    ln2_var(b + 2)
            run(dve, step)


_INS = ["L0_attn_x", "L0_attn_Wq", "L0_attn_bq", "L0_attn_Wk", "L0_attn_bk", "L0_attn_Wv", "L0_attn_bv", "L0_attn_Wo",
        "L0_attn_bo", "L0_attn_ln_g", "L0_attn_ln_b", "L0_ffn_router_w", "L0_ffn_w_in", "L0_ffn_b_in", "L0_ffn_w_out",
        "L0_ffn_b_out", "L0_c", "L0_wmod"]


def kernel(**inputs):
    import numpy as np
    import concourse.bacc as bacc
    from concourse.bass_utils import run_bass_kernel_spmd

    nc = bacc.Bacc("TRN2", target_bir_lowering=False, num_devices=1)
    arrays, args = {}, []
    for name in _INS:
        a = np.ascontiguousarray(inputs[name])
        arrays[f"in_{name}"] = a
        args.append(nc.dram_tensor(f"in_{name}", a.shape, mybir.dt.from_np(a.dtype), kind="ExternalInput").ap())
    x_shape = arrays["in_L0_attn_x"].shape
    out = nc.dram_tensor("out", x_shape, F32, kind="ExternalOutput").ap()
    gate_scratch = nc.dram_tensor("gate_scratch", (x_shape[0], 2 * P), F32, kind="Internal").ap()
    adaln_block(nc, *args, out, gate_scratch)
    r = run_bass_kernel_spmd(nc, [arrays], core_ids=[0])
    return r.results[0]["out"]
```

```python
from contextlib import ExitStack

import concourse.bass as bass
from concourse import mybir

F32 = mybir.dt.float32
F32R = mybir.dt.float32r
ALU = mybir.AluOpType
ACT = mybir.ActivationFunctionType
AX = mybir.AxisListType

P = 128
LN_EPS = 1e-5
GATE_MIN = 0.25
HEAD_DIM = 8
DMA = 16


def adaln_block(nc, x, Wq, bq, Wk, bk, Wv, bv, Wo, bo, ln_g, ln_b, router_w, w_in, b_in, w_out, b_out, c, wmod, out, gate_scratch, route_scratch):
    NB, NTOK, C = x.shape
    T = NTOK // P
    NE = router_w.shape[1]
    HEADS = C // HEAD_DIM
    NMOD = wmod.shape[1] // C
    ROW = 32
    U = 4
    ON_POOL = (1, 3)
    PARTS = 4
    assert C == P and NTOK == 512 and NE == 8 and w_in.shape[2] == P and NMOD == 6

    x_v = x.rearrange("b (p t) c -> b p (t c)", t=T)
    out_v = out.rearrange("b (p t) c -> b p (t c)", t=T)

    with ExitStack() as ctx:
        def sb(name, shape, dt=F32):
            return ctx.enter_context(nc.sbuf_tensor(name, shape, dt))

        def sem(name):
            return ctx.enter_context(nc.semaphore(name))

        ident = sb("ident", [P, P])
        ones_col = sb("ones_col", [P, 1])
        neg_half = sb("neg_half", [P, T])
        blockmask = sb("blockmask", [P, P])
        w_nat = sb("w_nat", [P, 4, P])
        wqv_hi = sb("wqv_hi", [P, 2, P], F32R)
        wqv_lo = sb("wqv_lo", [P, 2, P], F32R)
        wk_hi = sb("wk_hi", [P, P], F32R)
        wk_lo = sb("wk_lo", [P, P], F32R)
        woT = sb("woT", [P, P])
        wo_gain = sb("wo_gain", [P, P])
        NROW = NE + 3
        rows = sb("rows", [NROW, P])
        cols = sb("cols", [P, NROW])
        bo_bc = sb("bo_bc", [NB, P])
        bv_mask = sb("bv_mask", [P, P])
        bq_ld = sb("bq_ld", [33, P])
        bq_tmp = sb("bq_tmp", [33, P], F32R)
        bq_pad = sb("bq_pad", [P, P], F32R)
        bq_ones = sb("bq_ones", [P, P], F32R)
        bq_ones32 = sb("bq_ones32", [P, P])
        rw = sb("rw", [P, NE])
        win = sb("win", [P, NE, P])
        win_hi = sb("win_hi", [P, NE, P], F32R)
        win_lo = sb("win_lo", [P, NE, P], F32R)
        wout = sb("wout", [P, NE, P])
        bout_ld = sb("bout_ld", [2 * NE, P])
        bout_hi = sb("bout_hi", [P, P], F32R)
        bout_lo = sb("bout_lo", [P, P], F32R)
        c_sb = sb("c_sb", [NB, P])
        silu_c = sb("silu_c", [NB, P])
        silu_cT = sb("silu_cT", [P, NB])
        wmod_sb = sb("wmod_sb", [P, NMOD, P])
        modT = sb("modT", [P, NB, 5])
        gsign_b = sb("gsign_b", [P, NB])
        gabs_b = sb("gabs_b", [P, NB])
        gsign_a = sb("gsign_a", [NB, P])
        gabs_a = sb("gabs_a", [NB, P])
        ga_rows = sb("ga_rows", [NB, 2, P])
        lnb_bc = sb("lnb_bc", [P, NB])
        attn_const = sb("attn_const", [NB, P])
        gates = sb("gates", [P, NB, 2, P])

        x_all = sb("x_all", [P, NB, T, P])
        st1 = sb("st1", [P, T, 6])
        mv1 = sb("mv1", [P, T, 2])
        ve1 = sb("ve1", [P, T])
        rstd1 = sb("rstd1", [P, T])
        xn1 = sb("xn1", [P, T, P])
        modA = sb("modA", [P, 2])
        h = sb("h", [P, NTOK])
        h_hi = sb("h_hi", [P, NTOK], F32R)
        h_lo = sb("h_lo", [P, NTOK], F32R)
        kmax = sb("kmax", [P, 1])
        kbmax = sb("kbmax", [P, 1])
        kshift = sb("kshift", [P, 1])
        ekT = sb("ekT", [P, NTOK])
        ksum = sb("ksum", [P, 1])
        kinv = sb("kinv", [P, 1])
        ek = sb("ek", [P, T, P])
        qmax = sb("qmax", [P, T * HEADS])
        qs = sb("qs", [P, T * HEADS, HEAD_DIM])
        eq = sb("eq", [P, T * HEADS, HEAD_DIM])
        qsum = sb("qsum", [P, T * HEADS])
        qinv = sb("qinv", [P, T * HEADS])
        qn = sb("qn", [P, T * HEADS, HEAD_DIM])
        qT = sb("qT", [P, NTOK])
        v_sb = sb("v_sb", [P, T, P])
        s1 = sb("s1", [P, P])
        s2 = sb("s2", [P, P])
        srow = sb("srow", [P, 1])
        smean = sb("smean", [P, 1])
        s3 = sb("s3", [P, P])
        outT = sb("outT", [P, NTOK])
        sq = sb("sq", [P, NTOK])
        wog = sb("wog", [P, P])
        ve_o = sb("ve_o", [P, T])
        rstd_o = sb("rstd_o", [P, T])
        st2 = sb("st2", [P, T, 6])
        mv2 = sb("mv2", [P, T, 2])
        ve2 = sb("ve2", [P, T])
        rstd2 = sb("rstd2", [P, T])
        xn2 = sb("xn2", [P, T, P])
        modB = sb("modB", [P, 2, 2])
        modG = sb("modG", [P, 2, 1])
        h2 = sb("h2", [P, NTOK])
        h2_hi = sb("h2_hi", [P, 2, NTOK], F32R)
        h2_lo = sb("h2_lo", [P, 2, NTOK], F32R)
        lg = sb("lg", [P, T, NE])
        top = sb("top", [P, T, 8])
        top2 = sb("top2", [P, T, 8])
        lg_cut = sb("lg_cut", [P, T, NE])
        lshift = sb("lshift", [P, T, NE])
        elg = sb("elg", [P, T, NE])
        esum = sb("esum", [P, T])
        einv = sb("einv", [P, T])
        chosen = sb("chosen", [P, T, NE])
        echosen = sb("echosen", [P, T, NE])
        gate_hi = sb("gate_hi", [P, T, NE], F32R)
        gate2 = sb("gate2", [P, T, P])
        gateT = sb("gateT", [P, 2, NTOK], F32R)
        gate_rows = sb("gate_rows", [ROW + NE, NTOK])
        gate_bc = sb("gate_bc", [P, 2, NE, NTOK])
        u = sb("u", [P, U, NTOK])
        v = sb("v", [P, U, NTOK])
        yg = sb("yg", [P, NTOK])

        pH = ctx.enter_context(nc.psum_tensor("pH", [P, 2, NTOK], F32))
        pC = ctx.enter_context(nc.psum_tensor("pC", [P, NTOK], F32))
        pY = ctx.enter_context(nc.psum_tensor("pY", [P, NTOK], F32))
        pB = ctx.enter_context(nc.psum_tensor("pB", [P, NTOK], F32))
        pQV = ctx.enter_context(nc.psum_tensor("pQV", [P, T, 2, P], F32))
        pA = ctx.enter_context(nc.psum_tensor("pA", [P, NTOK], F32))
        pQV_flat = pQV[:, :, :, :].rearrange("p t w c -> p (t w c)")
        pQT = pQV_flat[:, 0:NTOK]
        pS = pC[:, 0:P]
        pSSQ = pB[:, T * NE:T * NE + T]
        q_view = pQV[:, :, 0, :].rearrange("p t (h d) -> p t h d", d=HEAD_DIM)

        s = {n: sem(n) for n in (
            "x_loaded loads_a loads_b const_set const_ready silu_ready tr_w tr_small cols_ready w_hi_ready prep_w mm_mod prep_mod "
            "mm_const rows_ready gates_stored gates_loaded prep_v prep_b prep_c  "
            "st1_done mv1_done ve1_done rstd1_ready xn1_ready "
            "hT_done modA_ready h_ready hhi_ready hlo_ready kT_done kmax_done kbmax_done kshift_ready ek_exp kinv_ready qv_done qmax_done qs_ready v_ready "
            "eq_ready qsum_done qinv_ready qn_ready ekT_done ek_ready qT_done qT_ready state_done s1_done s2_done smean_done s_ready out_done "
            "outT_ready sq_ready ssq_done veo_done rstdo_ready xg_ready wog_ready wo_done x1_ready st2_done mv2_done ve2_done rstd2_ready xn2_ready "
            "modB_ready h2T_done h2_ready h2hi_ready h2lo_ready logits_done lg_ready top_done top2_done cut_done lshift_ready elg_ready "
            "esum_done einv_done chosen_done echosen_done gate_done ghi_done gate2_ready gateT_done gateT_ready "
            "gf_ready row_stored modG_ready mm1_done gelu_done v_done vp_done mm2_done yg_ready yT_done out_ready stored"
        ).split() + [f"part{j}_{half}" for j in range(PARTS) for half in range(2)]}

        def w(eng, name, value):
            if not (isinstance(value, int) and value <= 0):
                eng.wait_ge(s[name], value)

        def weighed(b, e):
            if e < 0:
                b, e = b - 1, e + NE
            mine = [i for i in range(NE) if (i in ON_POOL) == (e in ON_POOL)]
            return "vp_done" if e in ON_POOL else "v_done", len(mine) * b + mine.index(e) + 1

        LOADS_A = 12
        LOADS_B = 7
        N_FULL = NB - 4

        def run(eng, step):
            for b in (-4, -3, -2, -1, 0):
                step(b, b % 2)
            with eng.Fori(1, N_FULL - 2, 2) as i:
                step(i, 1)
                step(i + 1, 0)
            for b in range(N_FULL - 1, NB + 1):
                step(b, b % 2)

        def has(b, stage):
            return not isinstance(b, int) or 0 <= b + stage < NB

        block = ctx.enter_context(nc.Block())

        @block.sync
        def _(sp):
            sp.dma_start(x_all[:, 0, :, :], x_v[0]).then_inc(s["x_loaded"], DMA)

            def spread_mod_gates():
                sp.wait_ge(s["rows_ready"], 3)
                sp.dma_start(gate_scratch, ga_rows[:, :, :].rearrange("b w c -> b (w c)")).then_inc(s["gates_stored"], DMA)
                sp.wait_ge(s["gates_stored"], DMA)
                sp.dma_start(gates[:, :, :, :].rearrange("p b w c -> p (b w c)"),
                             gate_scratch.rearrange("(a b) n -> a (b n)", a=1).to_broadcast([P, NB * 2 * P])).then_inc(s["gates_loaded"], DMA)

            def step(b, par):
                nxt = (par + 1) % 2
                if has(b, 5):
                    sp.wait_ge(s["x_loaded"], DMA * (b + 5))
                    sp.dma_start(x_all[:, b + 5, :, :], x_v[b + 5]).then_inc(s["x_loaded"], DMA)
                if isinstance(b, int) and b == -3:
                    spread_mod_gates()
                if has(b, -1):
                    sp.wait_ge(s["out_ready"], b)
                    sp.dma_start(out_v[b - 1], x_all[:, b - 1, :, :]).then_inc(s["stored"], DMA)
                if has(b, 1):
                    sp.wait_ge(s["gf_ready"], b + 2)
                    sp.dma_start(route_scratch[nxt], gate_rows[ROW:ROW + NE, :]).then_inc(s["row_stored"], DMA)
                    sp.wait_ge(s["row_stored"], DMA * (b + 2))
                    for j in range(PARTS):
                        es = slice(j * NE // PARTS, (j + 1) * NE // PARTS)
                        sp.dma_start(gate_bc[:, nxt, es, :].rearrange("p e n -> p (e n)"),
                                     route_scratch[nxt, es, :].rearrange("(a e) n -> a (e n)", a=1).to_broadcast([P, NE // PARTS * NTOK])
                                     ).then_inc(s[f"part{j}_{nxt}"], DMA)
            run(sp, step)
            sp.wait_ge(s["stored"], DMA * NB)

        @block.gpsimd
        def _(pool):
            pool.memset(ident[:, :], 0.0).then_inc(s["const_set"], 1)
            pool.memset(blockmask[:, :], 1.0).then_inc(s["const_set"], 1)
            pool.memset(neg_half[:, :], -0.5)
            pool.memset(ones_col[:, :], 1.0)
            pool.memset(gate2[:, :, :], 0.0)
            pool.memset(top2[:, :, :], 3.0e38).then_inc(s["const_set"], 1)
            pool.wait_ge(s["const_set"], 1)
            pool.affine_select(out=ident[:, :], in_=ident[:, :], compare_op=ALU.not_equal, fill=1.0, base=0,
                               pattern=[[-1, P]], channel_multiplier=1).then_inc(s["const_ready"], 1)
            pool.wait_ge(s["const_set"], 2)
            bm = blockmask[:, :].rearrange("p (h d) -> p h d", d=HEAD_DIM)
            pool.affine_select(out=bm, in_=bm, compare_op=ALU.is_ge, fill=0.0, base=0,
                               pattern=[[-HEAD_DIM, HEADS], [0, HEAD_DIM]], channel_multiplier=1).then_inc(s["const_set"], 1)
            pool.wait_ge(s["const_set"], 4)
            pool.affine_select(out=bm, in_=bm, compare_op=ALU.is_ge, fill=0.0, base=HEAD_DIM - 1,
                               pattern=[[HEAD_DIM, HEADS], [0, HEAD_DIM]], channel_multiplier=-1).then_inc(s["const_ready"], 1)

            def rstd_L(n):
                pool.wait_ge(s["ve1_done"], n + 1)
                pool.tensor_tensor(rstd1[:, :], ve1[:, :], neg_half[:, :], ALU.pow).then_inc(s["rstd1_ready"], 1)

            def mod_A(n):
                pool.tensor_copy(modA[:, :], modT[:, n, 0:2]).then_inc(s["modA_ready"], 1)

            def mod_B(n, par):
                w(pool, "h2hi_ready", n - 1)
                pool.tensor_copy(modB[:, par, :], modT[:, n, 2:4]).then_inc(s["modB_ready"], 1)

            def mod_G(b, par):
                w(pool, "yg_ready", b - 1)
                pool.tensor_copy(modG[:, par, :], modT[:, b, 4:5]).then_inc(s["modG_ready"], 1)

            def gated_const(n):
                pool.tensor_tensor(x_all[:, n, :, :], x_all[:, n, :, :],
                                   gates[:, n, 1, :].unsqueeze(1).to_broadcast([P, T, P]), ALU.add).then_inc(s["xg_ready"], 1)
                pool.tensor_tensor(wog[:, :], wo_gain[:, :], gates[:, n, 0, :], ALU.mult).then_inc(s["wog_ready"], 1)

            def rstd_O(n):
                pool.wait_ge(s["veo_done"], n + 1)
                pool.tensor_tensor(rstd_o[:, :], ve_o[:, :], neg_half[:, :], ALU.pow).then_inc(s["rstdo_ready"], 1)

            def h2_low(n, par):
                pool.wait_ge(s["h2hi_ready"], n + 1)
                pool.tensor_tensor(h2_lo[:, par, :], h2[:, :], h2_hi[:, par, :].bitcast(F32), ALU.subtract).then_inc(s["h2lo_ready"], 1)

            def weigh(b, par, e):
                pool.wait_ge(s["gelu_done"], NE * b + e + 1)
                pool.wait_ge(s[f"part{e * PARTS // NE}_{par}"], DMA // 2 * (b + 2 - par))
                w(pool, "mm2_done", NE * b + e - U + 1)
                pool.tensor_tensor(v[:, e % U, :], u[:, e % U, :], gate_bc[:, par, e, :], ALU.mult).then_inc(s["vp_done"], 1)

            def rstd_B(n):
                pool.wait_ge(s["ve2_done"], n + 1)
                pool.tensor_tensor(rstd2[:, :], ve2[:, :], neg_half[:, :], ALU.pow).then_inc(s["rstd2_ready"], 1)

            def step(b, par):
                Y, M, B, A2, A1, L = (has(b, k) for k in range(-1, 5))
                nxt = (par + 1) % 2
                if isinstance(b, int) and b == -3:
                    pool.wait_ge(s["prep_mod"], 5)
                if isinstance(b, int) and b == -2:
                    pool.wait_ge(s["gates_loaded"], DMA)
                    pool.wait_ge(s["prep_c"], 1)
                if B:
                    mod_B(b + 1, nxt)
                if M:
                    mod_G(b, par)
                if A1:
                    mod_A(b + 3)
                if L:
                    rstd_L(b + 4)
                if A2:
                    gated_const(b + 2)
                if M:
                    weigh(b, par, 1)
                if B:
                    h2_low(b + 1, nxt)
                if M:
                    weigh(b, par, 3)
                if A2:
                    rstd_O(b + 2)
                    rstd_B(b + 2)
            run(pool, step)

        @block.scalar
        def _(act):
            la, lb = s["loads_a"], s["loads_b"]
            act.dma_start(c_sb[:, :], c).then_inc(la, DMA)
            act.dma_start(wmod_sb[:, :, :], wmod.rearrange("k (j c) -> k j c", j=NMOD)).then_inc(la, DMA)
            for j, wt in enumerate((Wq, Wv, Wk, Wo)):
                act.dma_start(w_nat[:, j, :], wt).then_inc(la, DMA)
            act.dma_start(rows[0:NE, :], b_in).then_inc(la, DMA)
            for j, r in enumerate((bk, ln_g, ln_b)):
                act.dma_start(rows[NE + j:NE + j + 1, :], r.rearrange("(a n) -> a n", a=1)).then_inc(la, DMA)
            act.dma_start(bo_bc[:, :], bo.rearrange("(a n) -> a n", a=1).to_broadcast([NB, P])).then_inc(la, DMA)
            act.dma_start(bv_mask[:, :], bv.rearrange("(a n) -> a n", a=1).to_broadcast([P, P])).then_inc(la, DMA)
            act.dma_start(bq_ld[0:1, :], bq.rearrange("(a n) -> a n", a=1)).then_inc(lb, DMA)
            act.dma_start(bq_ld[32:33, :], bq.rearrange("(a n) -> a n", a=1)).then_inc(lb, DMA)
            act.dma_start(rw[:, :], router_w).then_inc(lb, DMA)
            act.dma_start(win[:, :, :], w_in.rearrange("e d h -> d e h")).then_inc(lb, DMA)
            act.dma_start(wout[:, :, :], w_out.rearrange("e h d -> h e d")).then_inc(lb, DMA)
            act.dma_start(bout_ld[0:NE, :], b_out).then_inc(lb, DMA)
            act.dma_start(bout_ld[NE:2 * NE, :], b_out).then_inc(lb, DMA)
            act.wait_ge(la, DMA * LOADS_A)
            act.activation(silu_c[:, :], c_sb[:, :], ACT.Silu).then_inc(s["silu_ready"], 1)
            act.wait_ge(s["tr_w"], 4)
            act.activation(wqv_hi[:, :, :].rearrange("p a c -> p (a c)"), pQT[:, 0:2 * P], ACT.Copy).then_inc(s["w_hi_ready"], 1)
            act.activation(wk_hi[:, :], pQT[:, 2 * P:3 * P], ACT.Copy).then_inc(s["w_hi_ready"], 1)
            act.activation(woT[:, :], pQT[:, 3 * P:4 * P], ACT.Copy).then_inc(s["w_hi_ready"], 1)
            act.wait_ge(lb, DMA * LOADS_B)
            act.activation(win_hi[:, :, :], win[:, :, :], ACT.Copy).then_inc(s["w_hi_ready"], 1)

            def h_evac(n):
                act.wait_ge(s["hT_done"], n + 1)
                act.wait_ge(s["modA_ready"], n + 1)
                act.activation(h[:, :], pA[:, :], ACT.Identity, bias=modA[:, 1:2], scale=modA[:, 0:1]).then_inc(s["h_ready"], 1)
                act.activation(h_hi[:, :], pA[:, :], ACT.Identity, bias=modA[:, 1:2], scale=modA[:, 0:1]).then_inc(s["hhi_ready"], 1)

            def h2_evac(n, par):
                act.wait_ge(s["h2T_done"], n + 1)
                act.wait_ge(s["modB_ready"], n + 1)
                w(act, "h2lo_ready", n)
                act.activation(h2[:, :], pB[:, :], ACT.Identity, bias=modB[:, par, 1:2], scale=modB[:, par, 0:1]).then_inc(s["h2_ready"], 1)
                act.activation(h2_hi[:, par, :], pB[:, :], ACT.Identity, bias=modB[:, par, 1:2], scale=modB[:, par, 0:1]).then_inc(s["h2hi_ready"], 1)

            def exp_k(n):
                act.wait_ge(s["kshift_ready"], n + 1)
                act.activation(ekT[:, :], pA[:, :], ACT.Exp, bias=kshift[:, 0:1], accum_out=ksum[:, :]).then_inc(s["ek_exp"], 1)

            def exp_q(n):
                act.wait_ge(s["qs_ready"], n + 1)
                act.activation(eq[:, :, :], qs[:, :, :], ACT.Exp).then_inc(s["eq_ready"], 1)

            def exp_router(n):
                act.wait_ge(s["lshift_ready"], n + 1)
                act.activation(elg[:, :, :], lshift[:, :, :], ACT.Exp).then_inc(s["elg_ready"], 1)

            def ek_evac(n):
                act.wait_ge(s["ekT_done"], n + 1)
                act.activation(ek[:, :, :].rearrange("p t c -> p (t c)"), pA[:, :], ACT.Copy).then_inc(s["ek_ready"], 1)

            def qT_evac(n):
                act.wait_ge(s["qT_done"], n + 1)
                act.activation(qT[:, :], pQT, ACT.Copy).then_inc(s["qT_ready"], 1)

            def v_evac(n):
                act.wait_ge(s["qs_ready"], n + 1)
                act.activation(v_sb[:, :, :], pQV[:, :, 1, :], ACT.Copy).then_inc(s["v_ready"], 1)

            def outT_evac(n):
                act.wait_ge(s["out_done"], n + 1)
                act.activation(sq[:, :], pC[:, :], ACT.Square).then_inc(s["sq_ready"], 1)
                act.activation(outT[:, :], pC[:, :], ACT.Copy).then_inc(s["outT_ready"], 1)

            def gateT_evac(n, par):
                act.wait_ge(s["gateT_done"], n + 1)
                w(act, "row_stored", DMA * n)
                act.activation(gate_rows[ROW:ROW + NE, :], pB[ROW:ROW + NE, :], ACT.Copy).then_inc(s["gf_ready"], 1)
                act.activation(gateT[:, par, :], pB[:, :], ACT.Copy).then_inc(s["gateT_ready"], 1)

            def gelu(b, e):
                act.wait_ge(s["mm1_done"], NE * b + e + 1)
                w(act, *weighed(b, e - U))
                act.activation(u[:, e % U, :], pH[:, e % 2, :], ACT.Gelu_apprx_tanh, bias=cols[:, e:e + 1]).then_inc(s["gelu_done"], 1)

            def y_gate(b, par):
                act.wait_ge(s["mm2_done"], NE * (b + 1))
                act.wait_ge(s["modG_ready"], b + 1)
                act.activation(yg[:, :], pY[:, :], ACT.Copy, scale=modG[:, par, 0:1]).then_inc(s["yg_ready"], 1)

            def step(b, par):
                Y, M, B, A2, A1, L = (has(b, k) for k in range(-1, 5))
                nxt = (par + 1) % 2
                if M:
                    gelu(b, 0)
                if A1:
                    h_evac(b + 3)
                if B:
                    h2_evac(b + 1, nxt)
                if M:
                    gelu(b, 1)
                if Y:
                    y_gate(b - 1, nxt)
                if M:
                    gelu(b, 2)
                if A2:
                    outT_evac(b + 2)
                if M:
                    gelu(b, 3)
                if B:
                    exp_router(b + 1)
                if A1:
                    exp_k(b + 3)
                    exp_q(b + 3)
                    v_evac(b + 3)
                if M:
                    gelu(b, 4)
                    gelu(b, 5)
                if B:
                    gateT_evac(b + 1, nxt)
                if A1:
                    ek_evac(b + 3)
                if M:
                    gelu(b, 6)
                    gelu(b, 7)
                if A1:
                    qT_evac(b + 3)
            run(act, step)

        @block.tensor
        def _(pe):
            mm = pe.matmul
            pe.wait_ge(s["const_ready"], 1)
            pe.wait_ge(s["loads_a"], DMA * LOADS_A)
            for j in range(4):
                pe.transpose(pQT[:, j * P:(j + 1) * P], w_nat[:, j, :], ident[:, :]).then_inc(s["tr_w"], 1)
            pe.transpose(pA[:, 0:NROW], rows[:, :], ident[0:NROW, 0:NROW]).then_inc(s["tr_small"], 1)
            pe.wait_ge(s["silu_ready"], 1)
            pe.transpose(pH[:, 0, 0:NB], silu_c[:, :], ident[0:NB, 0:NB]).then_inc(s["tr_small"], 1)
            pe.wait_ge(s["cols_ready"], 3)
            for i, j in enumerate((1, 0, 4, 3, 5)):
                mm(pB[:, i * NB:(i + 1) * NB], wmod_sb[:, j, :], silu_cT[:, :], start=True, stop=True)
            mm(pY[0:NB, 0:P], silu_cT[:, :], wmod_sb[:, 2, :], start=True, stop=True)
            pe.wait_ge(s["w_hi_ready"], 3)
            mm(pY[0:NB, P:2 * P], lnb_bc[:, :], woT[:, :], start=True, stop=True).then_inc(s["mm_mod"], 1)
            pe.wait_ge(s["prep_w"], 7)

            def hT(n):
                pe.wait_ge(s["xn1_ready"], T * (n + 1))
                w(pe, "ek_ready", n)
                for t in range(T):
                    i = pe.transpose(pA[:, t * P:(t + 1) * P], xn1[:, t, :], ident[:, :])
                i.then_inc(s["hT_done"], 1)

            def kT(n):
                pe.wait_ge(s["hlo_ready"], n + 1)
                mm(pA[:, :], wk_hi[:, :], h_hi[:, :], start=True, stop=False)
                mm(pA[:, :], wk_lo[:, :], h_hi[:, :], start=False, stop=False)
                mm(pA[:, :], wk_hi[:, :], h_lo[:, :], start=False, stop=True).then_inc(s["kT_done"], 1)

            def qv(n):
                w(pe, "qT_ready", n)
                hi = wqv_hi[:, :, :].rearrange("p a c -> p (a c)")
                lo = wqv_lo[:, :, :].rearrange("p a c -> p (a c)")
                for t in range(T):
                    o = pQV[:, t, :, :].rearrange("p a c -> p (a c)")
                    ts = slice(t * P, (t + 1) * P)
                    mm(o, h_hi[:, ts], hi, start=True, stop=False)
                    mm(o, h_hi[:, ts], lo, start=False, stop=False)
                    mm(pQV[:, t, 0, :], bq_ones[:, :], bq_pad[:, :], start=False, stop=False)
                    i = mm(o, h_lo[:, ts], hi, start=False, stop=True)
                i.then_inc(s["qv_done"], 1)

            def ek_back(n):
                pe.wait_ge(s["ek_exp"], n + 1)
                for t in range(T):
                    i = pe.transpose(pA[:, t * P:(t + 1) * P], ekT[:, t * P:(t + 1) * P], ident[:, :])
                i.then_inc(s["ekT_done"], 1)

            def q_turn(n):
                pe.wait_ge(s["v_ready"], n + 1)
                pe.wait_ge(s["qn_ready"], n + 1)
                qf = qn[:, :, :].rearrange("p a d -> p (a d)")
                for t in range(T):
                    i = pe.transpose(pQT[:, t * P:(t + 1) * P], qf[:, t * P:(t + 1) * P], ident[:, :])
                i.then_inc(s["qT_done"], 1)

            def state(n):
                pe.wait_ge(s["v_ready"], n + 1)
                pe.wait_ge(s["ek_ready"], n + 1)
                w(pe, "x1_ready", T * n)
                for t in range(T):
                    i = mm(pS, ek[:, t, :], v_sb[:, t, :], start=(t == 0), stop=(t == T - 1))
                i.then_inc(s["state_done"], 1)

            def attend(n):
                pe.wait_ge(s["s_ready"], n + 1)
                pe.wait_ge(s["qT_ready"], n + 1)
                mm(pC[:, :], s3[:, :], qT[:, :], start=True, stop=True).then_inc(s["out_done"], 1)

            def ssq(n):
                pe.wait_ge(s["sq_ready"], n + 1)
                w(pe, "lg_ready", n)
                w(pe, "top_done", T * n)
                for t in range(T):
                    i = mm(pSSQ[:, t:t + 1], sq[:, t * P:(t + 1) * P], ones_col[:, :], start=True, stop=True)
                i.then_inc(s["ssq_done"], 1)

            def project(n):
                pe.wait_ge(s["outT_ready"], n + 1)
                pe.wait_ge(s["wog_ready"], n + 1)
                for t in range(T):
                    i = mm(pC[:, t * P:(t + 1) * P], outT[:, t * P:(t + 1) * P], wog[:, :], start=True, stop=True)
                i.then_inc(s["wo_done"], 1)

            def h2T(n):
                pe.wait_ge(s["xn2_ready"], T * (n + 1))
                w(pe, "gateT_ready", n)
                for t in range(T):
                    i = pe.transpose(pB[:, t * P:(t + 1) * P], xn2[:, t, :], ident[:, :])
                i.then_inc(s["h2T_done"], 1)

            def logits(n):
                pe.wait_ge(s["h2hi_ready"], n + 1)
                for t in range(T):
                    i = mm(pB[:, t * NE:(t + 1) * NE], h2[:, t * P:(t + 1) * P], rw[:, :], start=True, stop=True)
                i.then_inc(s["logits_done"], 1)

            def gate_turn(n):
                pe.wait_ge(s["gate2_ready"], n + 1)
                w(pe, "out_ready", n - 1)
                w(pe, "veo_done", n + 2 if not isinstance(n, int) else min(n + 2, NB))
                for t in range(T):
                    i = pe.transpose(pB[:, t * P:(t + 1) * P], gate2[:, t, :], ident[:, :])
                i.then_inc(s["gateT_done"], 1)

            def hidden(b, par, e):
                if e == 0:
                    pe.wait_ge(s["h2lo_ready"], b + 1)
                w(pe, "gelu_done", NE * b + e - 1)
                o = pH[:, e % 2, :]
                mm(o, win_hi[:, e, :], h2_hi[:, par, :], start=True, stop=False)
                mm(o, win_lo[:, e, :], h2_hi[:, par, :], start=False, stop=False)
                mm(o, win_hi[:, e, :], h2_lo[:, par, :], start=False, stop=True).then_inc(s["mm1_done"], 1)

            def combine(b, par, e):
                if e == 0:
                    pe.wait_ge(s["gateT_ready"], b + 1)
                    w(pe, "yg_ready", b)
                    mm(pY[:, :], bout_hi[:, :], gateT[:, par, :], start=True, stop=False)
                    mm(pY[:, :], bout_lo[:, :], gateT[:, par, :], start=False, stop=False)
                w(pe, *weighed(b, e))
                mm(pY[:, :], wout[:, e, :], v[:, e % U, :], start=False, stop=(e == NE - 1)).then_inc(s["mm2_done"], 1)

            def y_turn(b):
                clip = (lambda n: n) if not isinstance(b, int) else (lambda n: min(n, NB))
                pe.wait_ge(s["yg_ready"], b + 1)
                w(pe, "lg_ready", clip(b + 3))
                w(pe, "top_done", T * clip(b + 3))
                w(pe, "veo_done", clip(b + 4))
                for t in range(T):
                    i = pe.transpose(pB[:, t * P:(t + 1) * P], yg[:, t * P:(t + 1) * P], ident[:, :])
                i.then_inc(s["yT_done"], 1)

            def step(b, par):
                Y, M, B, A2, A1, L = (has(b, k) for k in range(-1, 5))
                nxt = (par + 1) % 2
                if M:
                    hidden(b, par, 0)
                if Y:
                    combine(b - 1, nxt, 6)
                if A1:
                    hT(b + 3)
                if B:
                    h2T(b + 1)
                if M:
                    hidden(b, par, 1)
                if Y:
                    combine(b - 1, nxt, 7)
                if A2:
                    state(b + 2)
                if M:
                    hidden(b, par, 2)
                if B:
                    logits(b + 1)
                if A1:
                    kT(b + 3)
                if M:
                    combine(b, par, 0)
                if A2:
                    attend(b + 2)
                if M:
                    hidden(b, par, 3)
                if A1:
                    qv(b + 3)
                if M:
                    combine(b, par, 1)
                    hidden(b, par, 4)
                if A2:
                    ssq(b + 2)
                    project(b + 2)
                if M:
                    combine(b, par, 2)
                if Y:
                    y_turn(b - 1)
                if M:
                    hidden(b, par, 5)
                    combine(b, par, 3)
                if A1:
                    ek_back(b + 3)
                if B:
                    gate_turn(b + 1)
                if M:
                    hidden(b, par, 6)
                    combine(b, par, 4)
                    hidden(b, par, 7)
                if A1:
                    q_turn(b + 3)
                if M:
                    combine(b, par, 5)
            run(pe, step)

        @block.vector
        def _(dve):
            dve.memset(bq_pad[:, :].bitcast(F32), 0.0)
            dve.memset(bq_ones32[:, :], 0.0)
            dve.memset(bout_hi[:, :].bitcast(F32), 0.0)
            dve.memset(bout_lo[:, :].bitcast(F32), 0.0).then_inc(s["prep_v"], 1)
            dve.wait_ge(s["prep_v"], 1)
            dve.memset(bq_ones32[0:1, :], 1.0)
            dve.memset(bq_ones32[32:33, :], 1.0).then_inc(s["prep_v"], 1)
            dve.wait_ge(s["prep_v"], 2)
            dve.tensor_copy(bq_ones[:, :], bq_ones32[:, :]).then_inc(s["prep_w"], 1)
            dve.wait_ge(s["tr_small"], 1)
            dve.tensor_copy(cols[:, :], pA[:, 0:NROW]).then_inc(s["cols_ready"], 1)
            dve.wait_ge(s["cols_ready"], 1)
            dve.tensor_copy(lnb_bc[:, :], cols[:, NE + 2:NE + 3].to_broadcast([P, NB])).then_inc(s["cols_ready"], 1)
            dve.wait_ge(s["tr_small"], 2)
            dve.tensor_copy(silu_cT[:, :], pH[:, 0, 0:NB]).then_inc(s["cols_ready"], 1)
            dve.wait_ge(s["w_hi_ready"], 3)
            dve.tensor_tensor(wqv_lo[:, :, :].rearrange("p a c -> p (a c)"), pQT[:, 0:2 * P],
                              wqv_hi[:, :, :].rearrange("p a c -> p (a c)").bitcast(F32), ALU.subtract).then_inc(s["prep_w"], 1)
            dve.tensor_tensor(wk_lo[:, :], pQT[:, 2 * P:3 * P], wk_hi[:, :].bitcast(F32), ALU.subtract).then_inc(s["prep_w"], 1)
            dve.tensor_scalar(wo_gain[:, :], woT[:, :], cols[:, NE + 1:NE + 2], None, ALU.mult).then_inc(s["prep_c"], 1)
            dve.wait_ge(s["mm_mod"], 1)
            pmod = pB[:, 0:5 * NB].rearrange("p (i b) -> p i b", b=NB)
            for i, plus in enumerate((1.0, 0.0, 1.0, 0.0)):
                dve.tensor_scalar(modT[:, :, i], pmod[:, i, :], plus, None, ALU.add).then_inc(s["prep_mod"], 1)

            def hold_gate(sign, mag, src, dst, done):
                dve.tensor_scalar(sign, src, 0.0, 2.0, ALU.is_ge, ALU.mult)
                dve.tensor_copy(mag, src).then_inc(s["prep_v"], 1)
                hold_gate.count += 1
                dve.wait_ge(s["prep_v"], hold_gate.count)
                dve.scalar_tensor_tensor(out=mag, in0=mag, scalar=-1.0, in1=src, op0=ALU.mult, op1=ALU.max).then_inc(s["prep_v"], 1)
                hold_gate.count += 1
                dve.wait_ge(s["prep_v"], hold_gate.count)
                dve.tensor_scalar(mag, mag, GATE_MIN, None, ALU.max).then_inc(s["prep_v"], 1)
                hold_gate.count += 1
                dve.wait_ge(s["prep_v"], hold_gate.count)
                dve.scalar_tensor_tensor(out=dst, in0=sign, scalar=-1.0, in1=mag, op0=ALU.add, op1=ALU.mult).then_inc(s[done], 1)
            hold_gate.count = 2
            hold_gate(gsign_b[:, :], gabs_b[:, :], pmod[:, 4, :], modT[:, :, 4], "prep_mod")
            hold_gate(gsign_a[:, :], gabs_a[:, :], pY[0:NB, 0:P], ga_rows[:, 0, :], "rows_ready")
            dve.tensor_tensor(attn_const[:, :], pY[0:NB, P:2 * P], bo_bc[:, :], ALU.add).then_inc(s["rows_ready"], 1)
            dve.wait_ge(s["rows_ready"], 2)
            dve.tensor_tensor(ga_rows[:, 1, :], ga_rows[:, 0, :], attn_const[:, :], ALU.mult).then_inc(s["rows_ready"], 1)
            dve.wait_ge(s["const_ready"], 2)
            dve.wait_ge(s["loads_a"], DMA * LOADS_A)
            dve.tensor_tensor(bv_mask[:, :], bv_mask[:, :], blockmask[:, :], ALU.mult).then_inc(s["prep_b"], 1)
            dve.wait_ge(s["loads_b"], DMA * LOADS_B)
            dve.tensor_copy(bq_pad[0:1, :], bq_ld[0:1, :]).then_inc(s["prep_w"], 1)
            dve.tensor_copy(bq_tmp[32:33, :], bq_ld[32:33, :])
            dve.tensor_copy(bout_hi[0:2 * NE, :], bout_ld[:, :]).then_inc(s["prep_v"], 1)
            dve.wait_ge(s["prep_v"], hold_gate.count + 1)
            dve.tensor_tensor(bq_pad[32:33, :], bq_ld[32:33, :], bq_tmp[32:33, :].bitcast(F32), ALU.subtract).then_inc(s["prep_w"], 1)
            dve.tensor_tensor(bout_lo[0:2 * NE, :], bout_ld[:, :], bout_hi[0:2 * NE, :].bitcast(F32), ALU.subtract).then_inc(s["prep_w"], 1)
            dve.wait_ge(s["w_hi_ready"], 4)
            dve.tensor_tensor(win_lo[:, :, :], win[:, :, :], win_hi[:, :, :].bitcast(F32), ALU.subtract).then_inc(s["prep_w"], 1)
            dve.wait_ge(s["prep_b"], 1)

            def x_here(n):
                dve.wait_ge(s["x_loaded"], DMA * (n + 1))

            def ln1_stats(n):
                for t in range(T):
                    dve.bn_stats(st1[:, t, :], x_all[:, n, t, :]).then_inc(s["st1_done"], 1)

            def ln1_stats_here(n):
                dve.wait_ge(s["st1_done"], T * n + T)

            def ln1_var(n):
                for t in range(T):
                    dve.bn_aggr(mv1[:, t, :], st1[:, t, :]).then_inc(s["mv1_done"], 1)
                dve.wait_ge(s["mv1_done"], T * n + T)
                dve.tensor_scalar(ve1[:, :], mv1[:, :, 1], LN_EPS, None, ALU.add).then_inc(s["ve1_done"], 1)

            def ln1_apply(n):
                dve.wait_ge(s["rstd1_ready"], n + 1)
                w(dve, "hT_done", n)
                for t in range(T):
                    dve.tensor_scalar(xn1[:, t, :], x_all[:, n, t, :], mv1[:, t, 0:1], rstd1[:, t:t + 1],
                                      ALU.subtract, ALU.mult).then_inc(s["xn1_ready"], 1)

            def h_low(n):
                dve.wait_ge(s["hhi_ready"], n + 1)
                dve.tensor_tensor(h_lo[:, :], h[:, :], h_hi[:, :].bitcast(F32), ALU.subtract).then_inc(s["hlo_ready"], 1)

            def k_max(n):
                dve.wait_ge(s["kT_done"], n + 1)
                dve.tensor_reduce(kmax[:, :], pA[:, :], AX.X, ALU.max).then_inc(s["kmax_done"], 1)
                dve.wait_ge(s["kmax_done"], n + 1)
                dve.tensor_tensor(kbmax[:, :], kmax[:, :], cols[:, NE:NE + 1], ALU.add).then_inc(s["kbmax_done"], 1)
                dve.wait_ge(s["kbmax_done"], n + 1)
                dve.tensor_tensor(kshift[:, :], cols[:, NE:NE + 1], kbmax[:, :], ALU.subtract).then_inc(s["kshift_ready"], 1)

            def q_shift(n):
                dve.wait_ge(s["qv_done"], n + 1)
                dve.tensor_reduce(qmax[:, :].rearrange("p (t h) -> p t h", t=T), q_view, AX.X, ALU.max).then_inc(s["qmax_done"], 1)
                dve.wait_ge(s["qmax_done"], n + 1)
                dve.tensor_tensor(qs[:, :, :].rearrange("p (t h) d -> p t h d", t=T), q_view,
                                  qmax[:, :].rearrange("p (t h) -> p t h", t=T).unsqueeze(3).to_broadcast([P, T, HEADS, HEAD_DIM]),
                                  ALU.subtract).then_inc(s["qs_ready"], 1)

            def q_sum(n):
                dve.wait_ge(s["eq_ready"], n + 1)
                dve.tensor_reduce(qsum[:, :], eq[:, :, :], AX.X, ALU.add).then_inc(s["qsum_done"], 1)
                dve.wait_ge(s["qsum_done"], n + 1)
                dve.reciprocal(qinv[:, :], qsum[:, :]).then_inc(s["qinv_ready"], 1)

            def q_norm(n):
                dve.wait_ge(s["qinv_ready"], n + 1)
                dve.tensor_tensor(qn[:, :, :], eq[:, :, :], qinv[:, :].unsqueeze(2).to_broadcast([P, T * HEADS, HEAD_DIM]),
                                   ALU.mult).then_inc(s["qn_ready"], 1)

            def k_inv(n):
                dve.wait_ge(s["ek_exp"], n + 1)
                dve.reciprocal(kinv[:, :], ksum[:, :]).then_inc(s["kinv_ready"], 1)

            def state_out(n):
                dve.wait_ge(s["state_done"], n + 1)
                dve.wait_ge(s["kinv_ready"], n + 1)
                dve.scalar_tensor_tensor(out=s1[:, :], in0=pS, scalar=kinv[:, 0:1], in1=blockmask[:, :],
                                         op0=ALU.mult, op1=ALU.mult).then_inc(s["s1_done"], 1)
                dve.wait_ge(s["s1_done"], n + 1)
                dve.scalar_tensor_tensor(out=s2[:, :], in0=s1[:, :], scalar=1.0, in1=bv_mask[:, :], op0=ALU.mult, op1=ALU.add,
                                         accum_out=srow[:, :]).then_inc(s["s2_done"], 1)
                dve.wait_ge(s["s2_done"], n + 1)
                dve.tensor_scalar(smean[:, :], srow[:, :], -1.0 / C, None, ALU.mult).then_inc(s["smean_done"], 1)
                dve.wait_ge(s["smean_done"], n + 1)
                dve.tensor_scalar(s3[:, :], s2[:, :], smean[:, 0:1], None, ALU.add).then_inc(s["s_ready"], 1)

            def out_var(n):
                dve.wait_ge(s["ssq_done"], n + 1)
                dve.tensor_scalar(ve_o[:, :], pSSQ, 1.0 / C, LN_EPS, ALU.mult, ALU.add).then_inc(s["veo_done"], 1)

            def residual1(n):
                dve.wait_ge(s["wo_done"], n + 1)
                dve.wait_ge(s["rstdo_ready"], n + 1)
                dve.wait_ge(s["xg_ready"], n + 1)
                for t in range(T):
                    dve.scalar_tensor_tensor(out=x_all[:, n, t, :], in0=pC[:, t * P:(t + 1) * P], scalar=rstd_o[:, t:t + 1],
                                             in1=x_all[:, n, t, :], op0=ALU.mult, op1=ALU.add).then_inc(s["x1_ready"], 1)

            def x1_here(n):
                dve.wait_ge(s["x1_ready"], T * n + T)

            def ln2_stats(n):
                for t in range(T):
                    dve.bn_stats(st2[:, t, :], x_all[:, n, t, :]).then_inc(s["st2_done"], 1)

            def ln2_stats_here(n):
                dve.wait_ge(s["st2_done"], T * n + T)

            def ln2_var(n):
                for t in range(T):
                    dve.bn_aggr(mv2[:, t, :], st2[:, t, :]).then_inc(s["mv2_done"], 1)
                dve.wait_ge(s["mv2_done"], T * n + T)
                dve.tensor_scalar(ve2[:, :], mv2[:, :, 1], LN_EPS, None, ALU.add).then_inc(s["ve2_done"], 1)

            def ln2_apply(n):
                dve.wait_ge(s["rstd2_ready"], n + 1)
                w(dve, "h2T_done", n)
                for t in range(T):
                    dve.tensor_scalar(xn2[:, t, :], x_all[:, n, t, :], mv2[:, t, 0:1], rstd2[:, t:t + 1],
                                      ALU.subtract, ALU.mult).then_inc(s["xn2_ready"], 1)

            def route(n):
                dve.wait_ge(s["logits_done"], n + 1)
                dve.tensor_copy(lg[:, :, :].rearrange("p t e -> p (t e)"), pB[:, 0:T * NE]).then_inc(s["lg_ready"], 1)
                for t in range(T):
                    dve.max(top[:, t, :], pB[:, t * NE:(t + 1) * NE]).then_inc(s["top_done"], 1)
                dve.wait_ge(s["top_done"], T * n + T)
                dve.tensor_copy(top2[:, :, 0:2], top[:, :, 0:2]).then_inc(s["top2_done"], 1)
                dve.wait_ge(s["lg_ready"], n + 1)
                dve.wait_ge(s["top2_done"], n + 1)
                dve.tensor_tensor(lshift[:, :, :], lg[:, :, :], top[:, :, 0:1].to_broadcast([P, T, NE]),
                                  ALU.subtract).then_inc(s["lshift_ready"], 1)
                for t in range(T):
                    dve.match_replace(lg_cut[:, t, :], top2[:, t, :], lg[:, t, :], -3.0e38).then_inc(s["cut_done"], 1)

            def gates_out(n):
                dve.wait_ge(s["cut_done"], T * n + T)
                dve.tensor_tensor(chosen[:, :, :], lg[:, :, :], lg_cut[:, :, :], ALU.not_equal).then_inc(s["chosen_done"], 1)
                dve.wait_ge(s["elg_ready"], n + 1)
                dve.tensor_reduce(esum[:, :], elg[:, :, :], AX.X, ALU.add).then_inc(s["esum_done"], 1)
                dve.wait_ge(s["chosen_done"], n + 1)
                dve.tensor_tensor(echosen[:, :, :], elg[:, :, :], chosen[:, :, :], ALU.mult).then_inc(s["echosen_done"], 1)
                dve.wait_ge(s["esum_done"], n + 1)
                dve.reciprocal(einv[:, :], esum[:, :]).then_inc(s["einv_done"], 1)
                dve.wait_ge(s["einv_done"], n + 1)
                w(dve, "gateT_done", n)
                gate = gate2[:, :, ROW:ROW + NE]
                dve.tensor_tensor(gate, echosen[:, :, :], einv[:, :].unsqueeze(2).to_broadcast([P, T, NE]),
                                  ALU.mult).then_inc(s["gate_done"], 1)
                dve.wait_ge(s["gate_done"], n + 1)
                dve.tensor_copy(gate_hi[:, :, :], gate).then_inc(s["ghi_done"], 1)
                dve.wait_ge(s["ghi_done"], n + 1)
                dve.tensor_copy(gate2[:, :, 0:NE], gate_hi[:, :, :].bitcast(F32))
                dve.tensor_tensor(gate2[:, :, NE:2 * NE], gate, gate_hi[:, :, :].bitcast(F32),
                                  ALU.subtract).then_inc(s["gate2_ready"], 1)

            def weigh(b, par, e):
                dve.wait_ge(s["gelu_done"], NE * b + e + 1)
                dve.wait_ge(s[f"part{e * PARTS // NE}_{par}"], DMA // 2 * (b + 2 - par))
                w(dve, "mm2_done", NE * b + e - U + 1)
                dve.tensor_tensor(v[:, e % U, :], u[:, e % U, :], gate_bc[:, par, e, :], ALU.mult).then_inc(s["v_done"], 1)

            def residual2(b):
                dve.wait_ge(s["yT_done"], b + 1)
                xb = x_all[:, b, :, :]
                dve.tensor_tensor(xb, pB[:, :].rearrange("p (t c) -> p t c", t=T), xb, ALU.add).then_inc(s["out_ready"], 1)

            def step(b, par):
                Y, M, B, A2, A1, L = (has(b, k) for k in range(-1, 5))
                nxt = (par + 1) % 2
                if L:
                    x_here(b + 4)
                if Y:
                    weigh(b - 1, nxt, 7)
                if L:
                    ln1_stats(b + 4)
                    ln1_stats_here(b + 4)
                if A1:
                    h_low(b + 3)
                if L:
                    ln1_var(b + 4)
                if M:
                    weigh(b, par, 0)
                if A2:
                    state_out(b + 2)
                if L:
                    ln1_apply(b + 4)
                if B:
                    route(b + 1)
                if A1:
                    k_max(b + 3)
                if M:
                    weigh(b, par, 2)
                if A1:
                    q_shift(b + 3)
                if A2:
                    out_var(b + 2)
                if B:
                    gates_out(b + 1)
                if A2:
                    residual1(b + 2)
                    x1_here(b + 2)
                if Y:
                    residual2(b - 1)
                if A1:
                    k_inv(b + 3)
                if M:
                    weigh(b, par, 4)
                if A2:
                    ln2_stats(b + 2)
                    ln2_stats_here(b + 2)
                if A1:
                    q_sum(b + 3)
                    q_norm(b + 3)
                if A2:
                    ln2_var(b + 2)
                if M:
                    weigh(b, par, 5)
                    weigh(b, par, 6)
                if A2:
                    ln2_apply(b + 2)
            run(dve, step)


_INS = ["L0_attn_x", "L0_attn_Wq", "L0_attn_bq", "L0_attn_Wk", "L0_attn_bk", "L0_attn_Wv", "L0_attn_bv", "L0_attn_Wo",
        "L0_attn_bo", "L0_attn_ln_g", "L0_attn_ln_b", "L0_ffn_router_w", "L0_ffn_w_in", "L0_ffn_b_in", "L0_ffn_w_out",
        "L0_ffn_b_out", "L0_c", "L0_wmod"]


def kernel(**inputs):
    import numpy as np
    import concourse.bacc as bacc
    from concourse.bass_utils import run_bass_kernel_spmd

    nc = bacc.Bacc("TRN2", target_bir_lowering=False, num_devices=1)
    arrays, args = {}, []
    for name in _INS:
        a = np.ascontiguousarray(inputs[name])
        arrays[f"in_{name}"] = a
        args.append(nc.dram_tensor(f"in_{name}", a.shape, mybir.dt.from_np(a.dtype), kind="ExternalInput").ap())
    x_shape = arrays["in_L0_attn_x"].shape
    out = nc.dram_tensor("out", x_shape, F32, kind="ExternalOutput").ap()
    gate_scratch = nc.dram_tensor("gate_scratch", (x_shape[0], 2 * P), F32, kind="Internal").ap()
    route_scratch = nc.dram_tensor("route_scratch", (2, arrays["in_L0_ffn_router_w"].shape[1], 4 * P), F32, kind="Internal").ap()
    adaln_block(nc, *args, out, gate_scratch, route_scratch)
    r = run_bass_kernel_spmd(nc, [arrays], core_ids=[0])
    return r.results[0]["out"]
```

```python
from contextlib import ExitStack

import concourse.bass as bass
from concourse import mybir

F32 = mybir.dt.float32
F32R = mybir.dt.float32r
ALU = mybir.AluOpType
ACT = mybir.ActivationFunctionType
AX = mybir.AxisListType

P = 128
LN_EPS = 1e-5
GATE_MIN = 0.25
HEAD_DIM = 8
DMA = 16


def adaln_block(nc, x, Wq, bq, Wk, bk, Wv, bv, Wo, bo, ln_g, ln_b, router_w, w_in, b_in, w_out, b_out, c, wmod, out, gate_scratch, route_scratch):
    NB, NTOK, C = x.shape
    T = NTOK // P
    NE = router_w.shape[1]
    HEADS = C // HEAD_DIM
    NMOD = wmod.shape[1] // C
    ROW = 32
    U = 4
    ON_POOL = (1, 3, 5)
    LOW_ON_POOL = (0, 1, 4)
    FINE = (0, 1, 4, 5)
    PARTS = 4
    assert C == P and NTOK == 512 and NE == 8 and w_in.shape[2] == P and NMOD == 6

    x_v = x.rearrange("b (p t) c -> b p (t c)", t=T)
    out_v = out.rearrange("b (p t) c -> b p (t c)", t=T)

    with ExitStack() as ctx:
        def sb(name, shape, dt=F32):
            return ctx.enter_context(nc.sbuf_tensor(name, shape, dt))

        def sem(name):
            return ctx.enter_context(nc.semaphore(name))

        ident = sb("ident", [P, P])
        ones_col = sb("ones_col", [P, 1])
        neg_half = sb("neg_half", [P, T])
        blockmask = sb("blockmask", [P, P])
        w_nat = sb("w_nat", [P, 4, P])
        wqv_hi = sb("wqv_hi", [P, 2, P], F32R)
        wqv_lo = sb("wqv_lo", [P, 2, P], F32R)
        wk_hi = sb("wk_hi", [P, P], F32R)
        wk_lo = sb("wk_lo", [P, P], F32R)
        woT = sb("woT", [P, P])
        wo_gain = sb("wo_gain", [P, P])
        NROW = NE + 3
        rows = sb("rows", [NROW, P])
        cols = sb("cols", [P, NROW])
        bo_bc = sb("bo_bc", [NB, P])
        bv_mask = sb("bv_mask", [P, P])
        bq_bc = sb("bq_bc", [P, P])
        rw = sb("rw", [P, NE])
        win = sb("win", [P, NE, P])
        win_hi = sb("win_hi", [P, NE, P], F32R)
        win_lo = sb("win_lo", [P, NE, P], F32R)
        wout = sb("wout", [P, NE, P])
        wout_hi = sb("wout_hi", [P, len(FINE), P], F32R)
        wout_lo = sb("wout_lo", [P, len(FINE), P], F32R)
        bout_ld = sb("bout_ld", [4 * NE, P])
        bout_hi = sb("bout_hi", [4 * NE, P], F32R)
        bout_part = sb("bout_part", [4 * NE, P])
        bout = sb("bout", [P, P], F32R)
        low_row = sb("low_row", [4 * NE, 1])
        high_row = sb("high_row", [4 * NE, 1])
        c_sb = sb("c_sb", [NB, P])
        silu_c = sb("silu_c", [NB, P])
        silu_cT = sb("silu_cT", [P, NB])
        wmod_sb = sb("wmod_sb", [P, NMOD, P])
        modT = sb("modT", [P, NB, 5])
        gsign_b = sb("gsign_b", [P, NB])
        gabs_b = sb("gabs_b", [P, NB])
        gsign_a = sb("gsign_a", [NB, P])
        gabs_a = sb("gabs_a", [NB, P])
        ga_rows = sb("ga_rows", [NB, 2, P])
        lnb_bc = sb("lnb_bc", [P, NB])
        attn_const = sb("attn_const", [NB, P])
        gates = sb("gates", [P, NB, 2, P])

        x_all = sb("x_all", [P, NB, T, P])
        st1 = sb("st1", [P, T, 6])
        mv1 = sb("mv1", [P, T, 2])
        ve1 = sb("ve1", [P, T])
        rstd1 = sb("rstd1", [P, T])
        xn1 = sb("xn1", [P, T, P])
        modA = sb("modA", [P, 2])
        h = sb("h", [P, NTOK])
        h_hi = sb("h_hi", [P, NTOK], F32R)
        h_lo = sb("h_lo", [P, NTOK], F32R)
        kmax = sb("kmax", [P, 1])
        kbmax = sb("kbmax", [P, 1])
        kshift = sb("kshift", [P, 1])
        ekT = sb("ekT", [P, NTOK])
        ksum = sb("ksum", [P, 1])
        kinv = sb("kinv", [P, 1])
        ek = sb("ek", [P, T, P])
        qmax = sb("qmax", [P, T * HEADS])
        qs = sb("qs", [P, T * HEADS, HEAD_DIM])
        eq = sb("eq", [P, T * HEADS, HEAD_DIM])
        qsum = sb("qsum", [P, T * HEADS])
        qinv = sb("qinv", [P, T * HEADS])
        qn = sb("qn", [P, T * HEADS, HEAD_DIM])
        qT = sb("qT", [P, NTOK])
        v_sb = sb("v_sb", [P, T, P])
        s1 = sb("s1", [P, P])
        s2 = sb("s2", [P, P])
        srow = sb("srow", [P, 1])
        smean = sb("smean", [P, 1])
        s3 = sb("s3", [P, P])
        outT = sb("outT", [P, NTOK])
        sq = sb("sq", [P, NTOK])
        wog = sb("wog", [P, P])
        ve_o = sb("ve_o", [P, T])
        rstd_o = sb("rstd_o", [P, T])
        st2 = sb("st2", [P, T, 6])
        mv2 = sb("mv2", [P, T, 2])
        ve2 = sb("ve2", [P, T])
        rstd2 = sb("rstd2", [P, T])
        xn2 = sb("xn2", [P, T, P])
        modB = sb("modB", [P, 2, 2])
        modG = sb("modG", [P, 2, 1])
        h2 = sb("h2", [P, NTOK])
        h2_hi = sb("h2_hi", [P, 2, NTOK], F32R)
        h2_lo = sb("h2_lo", [P, 2, NTOK], F32R)
        lg = sb("lg", [P, T, NE])
        top = sb("top", [P, T, 8])
        top2 = sb("top2", [P, T, 8])
        lg_cut = sb("lg_cut", [P, T, NE])
        lshift = sb("lshift", [P, T, NE])
        elg = sb("elg", [P, T, NE])
        esum = sb("esum", [P, T])
        einv = sb("einv", [P, T])
        chosen = sb("chosen", [P, T, NE])
        echosen = sb("echosen", [P, T, NE])
        gate_hi = sb("gate_hi", [P, T, NE], F32R)
        gate2 = sb("gate2", [P, T, P])
        gateT = sb("gateT", [P, 2, NTOK], F32R)
        gate_rows = sb("gate_rows", [ROW + NE, NTOK])
        gate_bc = sb("gate_bc", [P, 2, NE, NTOK])
        u = sb("u", [P, U, NTOK])
        v = sb("v", [P, U, NTOK])
        v_hi = sb("v_hi", [P, 2, NTOK], F32R)
        v_lo = sb("v_lo", [P, 2, NTOK], F32R)
        yg = sb("yg", [P, NTOK])

        pH = ctx.enter_context(nc.psum_tensor("pH", [P, 2, NTOK], F32))
        pC = ctx.enter_context(nc.psum_tensor("pC", [P, NTOK], F32))
        pY = ctx.enter_context(nc.psum_tensor("pY", [P, NTOK], F32))
        pB = ctx.enter_context(nc.psum_tensor("pB", [P, NTOK], F32))
        pQV = ctx.enter_context(nc.psum_tensor("pQV", [P, T, 2, P], F32))
        pA = ctx.enter_context(nc.psum_tensor("pA", [P, NTOK], F32))
        pQV_flat = pQV[:, :, :, :].rearrange("p t w c -> p (t w c)")
        pQT = pQV_flat[:, 0:NTOK]
        pS = pC[:, 0:P]
        pSSQ = pB[:, T * NE:T * NE + T]

        s = {n: sem(n) for n in (
            "x_loaded c_loaded w_loaded rows_loaded bias_loaded experts_loaded const_set const_ready silu_ready tr_silu tr_w tr_rows siluT_ready cols_ready "
            "w_hi_ready attn_w_ready wo_gain_ready bv_ready mm_mod mm_ga prep_mod gate_steps ga_ready gates_stored gates_loaded "
            "win_hi_ready bout_steps expert_w_ready "
            "st1_done mv1_done ve1_done rstd1_ready xn1_ready "
            "hT_done modA_ready hhi_ready hlo_ready kT_done kmax_done kbmax_done kshift_ready ek_exp kinv_ready qv_done qb_ready qmax_done qs_ready v_ready "
            "eq_ready qsum_done qinv_ready qn_ready ekT_done ek_ready qT_done qT_ready state_done s1_done s2_done smean_done s_ready out_done "
            "outT_ready sq_ready ssq_done veo_done rstdo_ready xg_ready wog_ready wo_done x1_ready st2_done mv2_done ve2_done rstd2_ready xn2_ready "
            "modB_ready h2T_done h2hi_ready h2lo_ready logits_done lg_ready top_done top2_done cut_done lshift_ready elg_ready "
            "esum_done einv_done chosen_done gate_done ghi_done gate2_ready gateT_done gateT_ready "
            "gf_ready row_stored modG_ready mm1_done gelu_done v_done vp_done vhi_done vlo_done vlop_done mm2_done yg_ready yT_done out_ready stored"
        ).split() + [f"part{j}_{half}" for j in range(PARTS) for half in range(2)]}

        def w(eng, name, value):
            if not (isinstance(value, int) and value <= 0):
                eng.wait_ge(s[name], value)

        def weighed(b, e):
            if e < 0:
                b, e = b - 1, e + NE
            mine = [i for i in range(NE) if (i in ON_POOL) == (e in ON_POOL)]
            return "vp_done" if e in ON_POOL else "v_done", len(mine) * b + mine.index(e) + 1

        def fine_count(b, e):
            return len(FINE) * b + FINE.index(e) + 1

        def lowered(b, e):
            mine = [i for i in FINE if (i in LOW_ON_POOL) == (e in LOW_ON_POOL)]
            return "vlop_done" if e in LOW_ON_POOL else "vlo_done", len(mine) * b + mine.index(e) + 1

        def fine_before(b, e):
            i = FINE.index(e) - 2
            return NE * b + FINE[i] + 1 if i >= 0 else NE * (b - 1) + FINE[i] + 1

        N_FULL = NB - 4

        def run(eng, step, after={}):
            for b in (-4, -3, -2, -1, 0):
                step(b, b % 2)
                if b in after:
                    after[b]()
            with eng.Fori(1, N_FULL - 2, 2) as i:
                step(i, 1)
                step(i + 1, 0)
            for b in range(N_FULL - 1, NB + 1):
                step(b, b % 2)

        def has(b, stage):
            return not isinstance(b, int) or 0 <= b + stage < NB

        block = ctx.enter_context(nc.Block())

        @block.sync
        def _(sp):
            sp.dma_start(x_all[:, 0, :, :], x_v[0]).then_inc(s["x_loaded"], DMA)
            for j, wt in enumerate((Wq, Wv, Wk, Wo)):
                sp.dma_start(w_nat[:, j, :], wt).then_inc(s["w_loaded"], DMA)
            sp.dma_start(bq_bc[:, :], bq.rearrange("(a n) -> a n", a=1).to_broadcast([P, P])).then_inc(s["bias_loaded"], DMA)
            sp.dma_start(bo_bc[:, :], bo.rearrange("(a n) -> a n", a=1).to_broadcast([NB, P])).then_inc(s["bias_loaded"], DMA)
            sp.dma_start(bv_mask[:, :], bv.rearrange("(a n) -> a n", a=1).to_broadcast([P, P])).then_inc(s["bias_loaded"], DMA)

            def load_experts():
                sp.dma_start(rw[:, :], router_w).then_inc(s["experts_loaded"], DMA)
                sp.dma_start(win[:, :, :], w_in.rearrange("e d h -> d e h")).then_inc(s["experts_loaded"], DMA)
                sp.dma_start(wout[:, :, :], w_out.rearrange("e h d -> h e d")).then_inc(s["experts_loaded"], DMA)
                for row in range(0, 4 * NE, NE):
                    sp.dma_start(bout_ld[row:row + NE, :], b_out).then_inc(s["experts_loaded"], DMA)

            def spread_mod_gates():
                sp.wait_ge(s["ga_ready"], 3)
                sp.dma_start(gate_scratch, ga_rows[:, :, :].rearrange("b w c -> b (w c)")).then_inc(s["gates_stored"], DMA)
                sp.wait_ge(s["gates_stored"], DMA)
                sp.dma_start(gates[:, :, :, :].rearrange("p b w c -> p (b w c)"),
                             gate_scratch.rearrange("(a b) n -> a (b n)", a=1).to_broadcast([P, NB * 2 * P])).then_inc(s["gates_loaded"], DMA)

            def step(b, par):
                nxt = (par + 1) % 2
                if has(b, 5):
                    sp.wait_ge(s["x_loaded"], DMA * (b + 5))
                    sp.dma_start(x_all[:, b + 5, :, :], x_v[b + 5]).then_inc(s["x_loaded"], DMA)
                if isinstance(b, int) and b == -3:
                    spread_mod_gates()
                if has(b, -1):
                    sp.wait_ge(s["out_ready"], b)
                    sp.dma_start(out_v[b - 1], x_all[:, b - 1, :, :]).then_inc(s["stored"], DMA)
                if has(b, 1):
                    sp.wait_ge(s["gf_ready"], b + 2)
                    sp.dma_start(route_scratch[nxt], gate_rows[ROW:ROW + NE, :]).then_inc(s["row_stored"], DMA)
                    sp.wait_ge(s["row_stored"], DMA * (b + 2))
                    for j in range(PARTS):
                        es = slice(j * NE // PARTS, (j + 1) * NE // PARTS)
                        sp.dma_start(gate_bc[:, nxt, es, :].rearrange("p e n -> p (e n)"),
                                     route_scratch[nxt, es, :].rearrange("(a e) n -> a (e n)", a=1).to_broadcast([P, NE // PARTS * NTOK])
                                     ).then_inc(s[f"part{j}_{nxt}"], DMA)
            run(sp, step, after={-4: load_experts})
            sp.wait_ge(s["stored"], DMA * NB)

        @block.gpsimd
        def _(pool):
            pool.memset(neg_half[:, :], -0.5)
            pool.memset(ones_col[:, :], 1.0)
            pool.memset(ident[:, :], 0.0).then_inc(s["const_set"], 1)
            pool.wait_ge(s["const_set"], 1)
            pool.affine_select(out=ident[:, :], in_=ident[:, :], compare_op=ALU.not_equal, fill=1.0, base=0,
                               pattern=[[-1, P]], channel_multiplier=1).then_inc(s["const_ready"], 1)

            def masks():
                pool.memset(blockmask[:, :], 1.0).then_inc(s["const_set"], 1)
                pool.wait_ge(s["const_set"], 2)
                bm = blockmask[:, :].rearrange("p (h d) -> p h d", d=HEAD_DIM)
                pool.affine_select(out=bm, in_=bm, compare_op=ALU.is_ge, fill=0.0, base=0,
                                   pattern=[[-HEAD_DIM, HEADS], [0, HEAD_DIM]], channel_multiplier=1).then_inc(s["const_set"], 1)
                pool.wait_ge(s["const_set"], 3)
                pool.affine_select(out=bm, in_=bm, compare_op=ALU.is_ge, fill=0.0, base=HEAD_DIM - 1,
                                   pattern=[[HEAD_DIM, HEADS], [0, HEAD_DIM]], channel_multiplier=-1).then_inc(s["const_ready"], 1)
                pool.memset(gate2[:, :, :], 0.0)
                pool.memset(top2[:, :, :], 3.0e38).then_inc(s["const_ready"], 1)

            def expert_parts():
                pool.wait_ge(s["win_hi_ready"], 1 + len(FINE))
                pool.tensor_tensor(win_lo[:, :, :], win[:, :, :], win_hi[:, :, :].bitcast(F32), ALU.subtract).then_inc(s["expert_w_ready"], 1)
                for i, e in enumerate(FINE):
                    pool.tensor_tensor(wout_lo[:, i, :], wout[:, e, :], wout_hi[:, i, :].bitcast(F32), ALU.subtract).then_inc(s["expert_w_ready"], 1)

            def rstd_L(n):
                pool.wait_ge(s["ve1_done"], n + 1)
                pool.tensor_tensor(rstd1[:, :], ve1[:, :], neg_half[:, :], ALU.pow).then_inc(s["rstd1_ready"], 1)

            def mod_A(n):
                pool.tensor_copy(modA[:, :], modT[:, n, 0:2]).then_inc(s["modA_ready"], 1)

            def mod_B(n, par):
                w(pool, "h2hi_ready", n - 1)
                pool.tensor_copy(modB[:, par, :], modT[:, n, 2:4]).then_inc(s["modB_ready"], 1)

            def mod_G(b, par):
                w(pool, "yg_ready", b - 1)
                pool.tensor_copy(modG[:, par, :], modT[:, b, 4:5]).then_inc(s["modG_ready"], 1)

            def gated_const(n):
                pool.tensor_tensor(x_all[:, n, :, :], x_all[:, n, :, :],
                                   gates[:, n, 1, :].unsqueeze(1).to_broadcast([P, T, P]), ALU.add).then_inc(s["xg_ready"], 1)
                pool.tensor_tensor(wog[:, :], wo_gain[:, :], gates[:, n, 0, :], ALU.mult).then_inc(s["wog_ready"], 1)

            def rstd_O(n):
                pool.wait_ge(s["veo_done"], n + 1)
                pool.tensor_tensor(rstd_o[:, :], ve_o[:, :], neg_half[:, :], ALU.pow).then_inc(s["rstdo_ready"], 1)

            def h2_low(n, par):
                pool.wait_ge(s["h2hi_ready"], n + 1)
                pool.tensor_tensor(h2_lo[:, par, :], h2[:, :], h2_hi[:, par, :].bitcast(F32), ALU.subtract).then_inc(s["h2lo_ready"], 1)

            def weigh(b, par, e):
                pool.wait_ge(s["gelu_done"], NE * b + e + 1)
                pool.wait_ge(s[f"part{e * PARTS // NE}_{par}"], DMA // 2 * (b + 2 - par))
                w(pool, "mm2_done", NE * b + e - U + 1)
                pool.tensor_tensor(v[:, e % U, :], u[:, e % U, :], gate_bc[:, par, e, :], ALU.mult).then_inc(s["vp_done"], 1)

            def v_low(b, e):
                pool.wait_ge(s["vhi_done"], fine_count(b, e))
                w(pool, "mm2_done", fine_before(b, e))
                i = FINE.index(e) % 2
                pool.tensor_tensor(v_lo[:, i, :], v[:, e % U, :], v_hi[:, i, :].bitcast(F32), ALU.subtract).then_inc(s["vlop_done"], 1)

            def h_low(n):
                pool.wait_ge(s["hhi_ready"], n + 1)
                pool.tensor_tensor(h_lo[:, :], h[:, :], h_hi[:, :].bitcast(F32), ALU.subtract).then_inc(s["hlo_ready"], 1)

            def rstd_B(n):
                pool.wait_ge(s["ve2_done"], n + 1)
                pool.tensor_tensor(rstd2[:, :], ve2[:, :], neg_half[:, :], ALU.pow).then_inc(s["rstd2_ready"], 1)

            def step(b, par):
                Y, M, B, A2, A1, L = (has(b, k) for k in range(-1, 5))
                nxt = (par + 1) % 2
                if isinstance(b, int) and b == -3:
                    pool.wait_ge(s["prep_mod"], 4)
                if isinstance(b, int) and b == -2:
                    pool.wait_ge(s["gates_loaded"], DMA)
                    pool.wait_ge(s["wo_gain_ready"], 1)
                if isinstance(b, int) and b == 0:
                    pool.wait_ge(s["prep_mod"], 5)
                if A1:
                    mod_A(b + 3)
                if B:
                    mod_B(b + 1, nxt)
                if A2:
                    gated_const(b + 2)
                if A1:
                    h_low(b + 3)
                if L:
                    rstd_L(b + 4)
                if M:
                    mod_G(b, par)
                    weigh(b, par, 1)
                    v_low(b, 0)
                if B:
                    h2_low(b + 1, nxt)
                if M:
                    v_low(b, 1)
                if A2:
                    rstd_O(b + 2)
                if M:
                    weigh(b, par, 3)
                    weigh(b, par, 5)
                    v_low(b, 4)
                if A2:
                    rstd_B(b + 2)
            run(pool, step, after={-4: masks, -3: expert_parts})

        @block.scalar
        def _(act):
            act.dma_start(c_sb[:, :], c).then_inc(s["c_loaded"], DMA)
            act.dma_start(wmod_sb[:, :, :], wmod.rearrange("k (j c) -> k j c", j=NMOD)).then_inc(s["c_loaded"], DMA)
            act.dma_start(rows[0:NE, :], b_in).then_inc(s["rows_loaded"], DMA)
            for j, r in enumerate((bk, ln_g, ln_b)):
                act.dma_start(rows[NE + j:NE + j + 1, :], r.rearrange("(a n) -> a n", a=1)).then_inc(s["rows_loaded"], DMA)
            act.wait_ge(s["c_loaded"], DMA * 2)
            act.activation(silu_c[:, :], c_sb[:, :], ACT.Silu).then_inc(s["silu_ready"], 1)
            act.wait_ge(s["tr_w"], 4)
            act.activation(wqv_hi[:, :, :].rearrange("p a c -> p (a c)"), pQT[:, 0:2 * P], ACT.Copy).then_inc(s["w_hi_ready"], 1)
            act.activation(wk_hi[:, :], pQT[:, 2 * P:3 * P], ACT.Copy).then_inc(s["w_hi_ready"], 1)
            act.activation(woT[:, :], pQT[:, 3 * P:4 * P], ACT.Copy).then_inc(s["w_hi_ready"], 1)

            def expert_parts():
                act.wait_ge(s["experts_loaded"], DMA * 7)
                act.activation(win_hi[:, :, :], win[:, :, :], ACT.Copy).then_inc(s["win_hi_ready"], 1)
                for i, e in enumerate(FINE):
                    act.activation(wout_hi[:, i, :], wout[:, e, :], ACT.Copy).then_inc(s["win_hi_ready"], 1)

            def h_evac(n):
                act.wait_ge(s["hT_done"], n + 1)
                act.wait_ge(s["modA_ready"], n + 1)
                act.activation(h[:, :], pA[:, :], ACT.Identity, bias=modA[:, 1:2], scale=modA[:, 0:1])
                act.activation(h_hi[:, :], pA[:, :], ACT.Identity, bias=modA[:, 1:2], scale=modA[:, 0:1]).then_inc(s["hhi_ready"], 1)

            def h2_evac(n, par):
                act.wait_ge(s["h2T_done"], n + 1)
                act.wait_ge(s["modB_ready"], n + 1)
                w(act, "h2lo_ready", n)
                act.activation(h2[:, :], pB[:, :], ACT.Identity, bias=modB[:, par, 1:2], scale=modB[:, par, 0:1])
                act.activation(h2_hi[:, par, :], pB[:, :], ACT.Identity, bias=modB[:, par, 1:2], scale=modB[:, par, 0:1]).then_inc(s["h2hi_ready"], 1)

            def exp_k(n):
                act.wait_ge(s["kshift_ready"], n + 1)
                act.activation(ekT[:, :], pA[:, :], ACT.Exp, bias=kshift[:, 0:1], accum_out=ksum[:, :]).then_inc(s["ek_exp"], 1)

            def exp_q(n):
                act.wait_ge(s["qs_ready"], n + 1)
                act.activation(eq[:, :, :], qs[:, :, :], ACT.Exp).then_inc(s["eq_ready"], 1)

            def exp_router(n):
                act.wait_ge(s["lshift_ready"], n + 1)
                act.activation(elg[:, :, :], lshift[:, :, :], ACT.Exp).then_inc(s["elg_ready"], 1)

            def ek_evac(n):
                act.wait_ge(s["ekT_done"], n + 1)
                act.activation(ek[:, :, :].rearrange("p t c -> p (t c)"), pA[:, :], ACT.Copy).then_inc(s["ek_ready"], 1)

            def qT_evac(n):
                act.wait_ge(s["qT_done"], n + 1)
                act.activation(qT[:, :], pQT, ACT.Copy).then_inc(s["qT_ready"], 1)

            def v_evac(n):
                act.wait_ge(s["qb_ready"], n + 1)
                act.activation(v_sb[:, :, :], pQV[:, :, 1, :], ACT.Copy).then_inc(s["v_ready"], 1)

            def outT_evac(n):
                act.wait_ge(s["out_done"], n + 1)
                act.activation(sq[:, :], pC[:, :], ACT.Square).then_inc(s["sq_ready"], 1)
                act.activation(outT[:, :], pC[:, :], ACT.Copy).then_inc(s["outT_ready"], 1)

            def gateT_evac(n, par):
                act.wait_ge(s["gateT_done"], n + 1)
                w(act, "row_stored", DMA * n)
                act.activation(gate_rows[ROW:ROW + NE, :], pB[ROW:ROW + NE, :], ACT.Copy).then_inc(s["gf_ready"], 1)
                act.activation(gateT[:, par, :], pB[:, :], ACT.Copy).then_inc(s["gateT_ready"], 1)

            def gelu(b, e):
                act.wait_ge(s["mm1_done"], NE * b + e + 1)
                w(act, *weighed(b, e - U))
                act.activation(u[:, e % U, :], pH[:, e % 2, :], ACT.Gelu_apprx_tanh, bias=cols[:, e:e + 1]).then_inc(s["gelu_done"], 1)

            def v_high(b, e):
                w(act, *weighed(b, e))
                w(act, "mm2_done", fine_before(b, e))
                act.activation(v_hi[:, FINE.index(e) % 2, :], v[:, e % U, :], ACT.Copy).then_inc(s["vhi_done"], 1)

            def y_gate(b, par):
                act.wait_ge(s["mm2_done"], NE * (b + 1))
                act.wait_ge(s["modG_ready"], b + 1)
                act.activation(yg[:, :], pY[:, :], ACT.Copy, scale=modG[:, par, 0:1]).then_inc(s["yg_ready"], 1)

            def step(b, par):
                Y, M, B, A2, A1, L = (has(b, k) for k in range(-1, 5))
                nxt = (par + 1) % 2
                if M:
                    gelu(b, 0)
                if A1:
                    h_evac(b + 3)
                if M:
                    gelu(b, 1)
                if B:
                    h2_evac(b + 1, nxt)
                if M:
                    gelu(b, 2)
                    v_high(b, 0)
                if Y:
                    y_gate(b - 1, nxt)
                if M:
                    gelu(b, 3)
                    v_high(b, 1)
                if A2:
                    outT_evac(b + 2)
                if A1:
                    exp_k(b + 3)
                if B:
                    exp_router(b + 1)
                if A1:
                    exp_q(b + 3)
                if M:
                    gelu(b, 4)
                    gelu(b, 5)
                if A1:
                    v_evac(b + 3)
                if M:
                    v_high(b, 4)
                if B:
                    gateT_evac(b + 1, nxt)
                if M:
                    v_high(b, 5)
                    gelu(b, 6)
                    gelu(b, 7)
                if A1:
                    ek_evac(b + 3)
                    qT_evac(b + 3)
            run(act, step, after={-4: expert_parts})

        @block.tensor
        def _(pe):
            mm = pe.matmul
            pe.wait_ge(s["const_ready"], 1)
            pe.wait_ge(s["silu_ready"], 1)
            pe.transpose(pH[:, 0, 0:NB], silu_c[:, :], ident[0:NB, 0:NB]).then_inc(s["tr_silu"], 1)
            pe.wait_ge(s["w_loaded"], DMA * 4)
            for j in range(4):
                pe.transpose(pQT[:, j * P:(j + 1) * P], w_nat[:, j, :], ident[:, :]).then_inc(s["tr_w"], 1)
            pe.wait_ge(s["rows_loaded"], DMA * 4)
            pe.transpose(pC[:, 0:NROW], rows[:, :], ident[0:NROW, 0:NROW]).then_inc(s["tr_rows"], 1)
            pe.wait_ge(s["siluT_ready"], 1)
            for i, j in enumerate((1, 0, 4, 3, 5)):
                m = mm(pB[:, i * NB:(i + 1) * NB], wmod_sb[:, j, :], silu_cT[:, :], start=True, stop=True)
            m.then_inc(s["mm_mod"], 1)
            mm(pY[0:NB, 0:P], silu_cT[:, :], wmod_sb[:, 2, :], start=True, stop=True)
            pe.wait_ge(s["cols_ready"], 2)
            pe.wait_ge(s["w_hi_ready"], 3)
            mm(pY[0:NB, P:2 * P], lnb_bc[:, :], woT[:, :], start=True, stop=True).then_inc(s["mm_ga"], 1)
            pe.wait_ge(s["attn_w_ready"], 2)

            def router_here():
                pe.wait_ge(s["experts_loaded"], DMA * 7)

            def experts_here():
                pe.wait_ge(s["expert_w_ready"], 2 + len(FINE))

            def hT(n):
                pe.wait_ge(s["xn1_ready"], T * (n + 1))
                w(pe, "ek_ready", n)
                for t in range(T):
                    i = pe.transpose(pA[:, t * P:(t + 1) * P], xn1[:, t, :], ident[:, :])
                i.then_inc(s["hT_done"], 1)

            def kT(n):
                pe.wait_ge(s["hlo_ready"], n + 1)
                mm(pA[:, :], wk_hi[:, :], h_hi[:, :], start=True, stop=False)
                mm(pA[:, :], wk_lo[:, :], h_hi[:, :], start=False, stop=False)
                mm(pA[:, :], wk_hi[:, :], h_lo[:, :], start=False, stop=True).then_inc(s["kT_done"], 1)

            def qv(n):
                w(pe, "qT_ready", n)
                hi = wqv_hi[:, :, :].rearrange("p a c -> p (a c)")
                lo = wqv_lo[:, :, :].rearrange("p a c -> p (a c)")
                for t in range(T):
                    o = pQV[:, t, :, :].rearrange("p a c -> p (a c)")
                    ts = slice(t * P, (t + 1) * P)
                    mm(o, h_hi[:, ts], hi, start=True, stop=False)
                    mm(o, h_hi[:, ts], lo, start=False, stop=False)
                    i = mm(o, h_lo[:, ts], hi, start=False, stop=True)
                i.then_inc(s["qv_done"], 1)

            def ek_back(n):
                pe.wait_ge(s["ek_exp"], n + 1)
                for t in range(T):
                    i = pe.transpose(pA[:, t * P:(t + 1) * P], ekT[:, t * P:(t + 1) * P], ident[:, :])
                i.then_inc(s["ekT_done"], 1)

            def q_turn(n):
                pe.wait_ge(s["v_ready"], n + 1)
                pe.wait_ge(s["qn_ready"], n + 1)
                qf = qn[:, :, :].rearrange("p a d -> p (a d)")
                for t in range(T):
                    i = pe.transpose(pQT[:, t * P:(t + 1) * P], qf[:, t * P:(t + 1) * P], ident[:, :])
                i.then_inc(s["qT_done"], 1)

            def state(n):
                pe.wait_ge(s["v_ready"], n + 1)
                pe.wait_ge(s["ek_ready"], n + 1)
                w(pe, "x1_ready", T * n)
                for t in range(T):
                    i = mm(pS, ek[:, t, :], v_sb[:, t, :], start=(t == 0), stop=(t == T - 1))
                i.then_inc(s["state_done"], 1)

            def attend(n):
                pe.wait_ge(s["s_ready"], n + 1)
                pe.wait_ge(s["qT_ready"], n + 1)
                mm(pC[:, :], s3[:, :], qT[:, :], start=True, stop=True).then_inc(s["out_done"], 1)

            def ssq(n):
                pe.wait_ge(s["sq_ready"], n + 1)
                w(pe, "lg_ready", n)
                w(pe, "top_done", T * n)
                for t in range(T):
                    i = mm(pSSQ[:, t:t + 1], sq[:, t * P:(t + 1) * P], ones_col[:, :], start=True, stop=True)
                i.then_inc(s["ssq_done"], 1)

            def project(n):
                pe.wait_ge(s["outT_ready"], n + 1)
                pe.wait_ge(s["wog_ready"], n + 1)
                for t in range(T):
                    i = mm(pC[:, t * P:(t + 1) * P], outT[:, t * P:(t + 1) * P], wog[:, :], start=True, stop=True)
                i.then_inc(s["wo_done"], 1)

            def h2T(n):
                pe.wait_ge(s["xn2_ready"], T * (n + 1))
                w(pe, "gateT_ready", n)
                for t in range(T):
                    i = pe.transpose(pB[:, t * P:(t + 1) * P], xn2[:, t, :], ident[:, :])
                i.then_inc(s["h2T_done"], 1)

            def logits(n):
                pe.wait_ge(s["h2hi_ready"], n + 1)
                for t in range(T):
                    i = mm(pB[:, t * NE:(t + 1) * NE], h2[:, t * P:(t + 1) * P], rw[:, :], start=True, stop=True)
                i.then_inc(s["logits_done"], 1)

            def gate_turn(n):
                pe.wait_ge(s["gate2_ready"], n + 1)
                w(pe, "out_ready", n - 1)
                w(pe, "veo_done", n + 2 if not isinstance(n, int) else min(n + 2, NB))
                for t in range(T):
                    i = pe.transpose(pB[:, t * P:(t + 1) * P], gate2[:, t, :], ident[:, :])
                i.then_inc(s["gateT_done"], 1)

            def hidden(b, par, e):
                if e == 0:
                    pe.wait_ge(s["h2lo_ready"], b + 1)
                w(pe, "gelu_done", NE * b + e - 1)
                o = pH[:, e % 2, :]
                mm(o, win_hi[:, e, :], h2_hi[:, par, :], start=True, stop=False)
                mm(o, win_lo[:, e, :], h2_hi[:, par, :], start=False, stop=False)
                mm(o, win_hi[:, e, :], h2_lo[:, par, :], start=False, stop=True).then_inc(s["mm1_done"], 1)

            def combine(b, par, e):
                if e == 0:
                    pe.wait_ge(s["gateT_ready"], b + 1)
                    w(pe, "yg_ready", b)
                    mm(pY[:, :], bout[:, :], gateT[:, par, :], start=True, stop=False)
                if e in FINE:
                    f = FINE.index(e)
                    w(pe, *lowered(b, e))
                    mm(pY[:, :], wout_hi[:, f, :], v_hi[:, f % 2, :], start=False, stop=False)
                    mm(pY[:, :], wout_lo[:, f, :], v_hi[:, f % 2, :], start=False, stop=False)
                    mm(pY[:, :], wout_hi[:, f, :], v_lo[:, f % 2, :], start=False, stop=(e == NE - 1)).then_inc(s["mm2_done"], 1)
                else:
                    w(pe, *weighed(b, e))
                    mm(pY[:, :], wout[:, e, :], v[:, e % U, :], start=False, stop=(e == NE - 1)).then_inc(s["mm2_done"], 1)

            def y_turn(b):
                clip = (lambda n: n) if not isinstance(b, int) else (lambda n: min(n, NB))
                pe.wait_ge(s["yg_ready"], b + 1)
                w(pe, "lg_ready", clip(b + 3))
                w(pe, "top_done", T * clip(b + 3))
                w(pe, "veo_done", clip(b + 4))
                for t in range(T):
                    i = pe.transpose(pB[:, t * P:(t + 1) * P], yg[:, t * P:(t + 1) * P], ident[:, :])
                i.then_inc(s["yT_done"], 1)

            def step(b, par):
                Y, M, B, A2, A1, L = (has(b, k) for k in range(-1, 5))
                nxt = (par + 1) % 2
                if M:
                    hidden(b, par, 0)
                if A1:
                    hT(b + 3)
                if A2:
                    state(b + 2)
                if M:
                    hidden(b, par, 1)
                if Y:
                    combine(b - 1, nxt, 5)
                if B:
                    h2T(b + 1)
                if M:
                    hidden(b, par, 2)
                if Y:
                    combine(b - 1, nxt, 6)
                    combine(b - 1, nxt, 7)
                if A1:
                    kT(b + 3)
                if M:
                    hidden(b, par, 3)
                if A2:
                    attend(b + 2)
                if B:
                    logits(b + 1)
                if A1:
                    qv(b + 3)
                if M:
                    hidden(b, par, 4)
                if A2:
                    ssq(b + 2)
                if A1:
                    ek_back(b + 3)
                if A2:
                    project(b + 2)
                if Y:
                    y_turn(b - 1)
                if M:
                    combine(b, par, 0)
                    hidden(b, par, 5)
                    combine(b, par, 1)
                    hidden(b, par, 6)
                if B:
                    gate_turn(b + 1)
                if M:
                    combine(b, par, 2)
                    combine(b, par, 3)
                    hidden(b, par, 7)
                    combine(b, par, 4)
                if A1:
                    q_turn(b + 3)
            run(pe, step, after={-2: router_here, -1: experts_here})

        @block.vector
        def _(dve):
            dve.memset(bout[:, :].bitcast(F32), 0.0)
            pmod = pB[:, 0:5 * NB].rearrange("p (i b) -> p i b", b=NB)

            def hold_gate(sign, mag, src, dst, done):
                dve.tensor_scalar(sign, src, 0.0, 2.0, ALU.is_ge, ALU.mult)
                dve.tensor_copy(mag, src).then_inc(s["gate_steps"], 1)
                hold_gate.count += 1
                dve.wait_ge(s["gate_steps"], hold_gate.count)
                dve.scalar_tensor_tensor(out=mag, in0=mag, scalar=-1.0, in1=src, op0=ALU.mult, op1=ALU.max).then_inc(s["gate_steps"], 1)
                hold_gate.count += 1
                dve.wait_ge(s["gate_steps"], hold_gate.count)
                dve.tensor_scalar(mag, mag, GATE_MIN, None, ALU.max).then_inc(s["gate_steps"], 1)
                hold_gate.count += 1
                dve.wait_ge(s["gate_steps"], hold_gate.count)
                dve.scalar_tensor_tensor(out=dst, in0=sign, scalar=-1.0, in1=mag, op0=ALU.add, op1=ALU.mult).then_inc(s[done], 1)
            hold_gate.count = 0

            def attention_parts():
                dve.wait_ge(s["tr_silu"], 1)
                dve.tensor_copy(silu_cT[:, :], pH[:, 0, 0:NB]).then_inc(s["siluT_ready"], 1)
                dve.wait_ge(s["tr_rows"], 1)
                dve.tensor_copy(cols[:, :], pC[:, 0:NROW]).then_inc(s["cols_ready"], 1)
                dve.wait_ge(s["cols_ready"], 1)
                dve.tensor_copy(lnb_bc[:, :], cols[:, NE + 2:NE + 3].to_broadcast([P, NB])).then_inc(s["cols_ready"], 1)
                dve.wait_ge(s["mm_mod"], 1)
                for i, plus in enumerate((1.0, 0.0, 1.0, 0.0)):
                    dve.tensor_scalar(modT[:, :, i], pmod[:, i, :], plus, None, ALU.add).then_inc(s["prep_mod"], 1)
                dve.wait_ge(s["w_hi_ready"], 3)
                dve.tensor_tensor(wqv_lo[:, :, :].rearrange("p a c -> p (a c)"), pQT[:, 0:2 * P],
                                  wqv_hi[:, :, :].rearrange("p a c -> p (a c)").bitcast(F32), ALU.subtract).then_inc(s["attn_w_ready"], 1)
                dve.tensor_tensor(wk_lo[:, :], pQT[:, 2 * P:3 * P], wk_hi[:, :].bitcast(F32), ALU.subtract).then_inc(s["attn_w_ready"], 1)
                dve.wait_ge(s["bias_loaded"], DMA * 3)
                dve.tensor_scalar(wo_gain[:, :], woT[:, :], cols[:, NE + 1:NE + 2], None, ALU.mult).then_inc(s["wo_gain_ready"], 1)
                dve.wait_ge(s["mm_ga"], 1)
                hold_gate(gsign_a[:, :], gabs_a[:, :], pY[0:NB, 0:P], ga_rows[:, 0, :], "ga_ready")
                dve.tensor_tensor(attn_const[:, :], pY[0:NB, P:2 * P], bo_bc[:, :], ALU.add).then_inc(s["ga_ready"], 1)
                dve.wait_ge(s["ga_ready"], 2)
                dve.tensor_tensor(ga_rows[:, 1, :], ga_rows[:, 0, :], attn_const[:, :], ALU.mult).then_inc(s["ga_ready"], 1)

            def state_parts():
                dve.wait_ge(s["const_ready"], 3)
                parity = ident[0:4 * NE, 0:4 * NE].rearrange("p (a w e) -> p w a e", w=2, e=NE)
                dve.tensor_reduce(high_row[:, :], parity[:, 0, :, :], AX.XY, ALU.add)
                dve.tensor_reduce(low_row[:, :], parity[:, 1, :, :], AX.XY, ALU.add)
                dve.tensor_tensor(bv_mask[:, :], bv_mask[:, :], blockmask[:, :], ALU.mult).then_inc(s["bv_ready"], 1)
                hold_gate(gsign_b[:, :], gabs_b[:, :], pmod[:, 4, :], modT[:, :, 4], "prep_mod")
                dve.wait_ge(s["bv_ready"], 1)

            def expert_parts():
                dve.wait_ge(s["experts_loaded"], DMA * 7)
                dve.tensor_copy(bout_hi[:, :], bout_ld[:, :]).then_inc(s["bout_steps"], 1)
                dve.wait_ge(s["bout_steps"], 1)
                dve.tensor_tensor(bout_part[:, :], bout_ld[:, :], bout_hi[:, :].bitcast(F32), ALU.subtract).then_inc(s["bout_steps"], 1)
                dve.wait_ge(s["bout_steps"], 2)
                dve.tensor_scalar(bout_part[:, :], bout_part[:, :], low_row[:, 0:1], None, ALU.mult).then_inc(s["bout_steps"], 1)
                dve.wait_ge(s["bout_steps"], 3)
                dve.scalar_tensor_tensor(out=bout[0:4 * NE, :], in0=bout_hi[:, :].bitcast(F32), scalar=high_row[:, 0:1],
                                         in1=bout_part[:, :], op0=ALU.mult, op1=ALU.add).then_inc(s["expert_w_ready"], 1)

            def x_here(n):
                dve.wait_ge(s["x_loaded"], DMA * (n + 1))

            def ln1_stats(n):
                for t in range(T):
                    dve.bn_stats(st1[:, t, :], x_all[:, n, t, :]).then_inc(s["st1_done"], 1)

            def ln1_stats_here(n):
                dve.wait_ge(s["st1_done"], T * n + T)

            def ln1_var(n):
                for t in range(T):
                    dve.bn_aggr(mv1[:, t, :], st1[:, t, :]).then_inc(s["mv1_done"], 1)
                dve.wait_ge(s["mv1_done"], T * n + T)
                dve.tensor_scalar(ve1[:, :], mv1[:, :, 1], LN_EPS, None, ALU.add).then_inc(s["ve1_done"], 1)

            def ln1_apply(n):
                dve.wait_ge(s["rstd1_ready"], n + 1)
                w(dve, "hT_done", n)
                for t in range(T):
                    dve.tensor_scalar(xn1[:, t, :], x_all[:, n, t, :], mv1[:, t, 0:1], rstd1[:, t:t + 1],
                                      ALU.subtract, ALU.mult).then_inc(s["xn1_ready"], 1)

            def k_max(n):
                dve.wait_ge(s["kT_done"], n + 1)
                dve.tensor_reduce(kmax[:, :], pA[:, :], AX.X, ALU.max).then_inc(s["kmax_done"], 1)
                dve.wait_ge(s["kmax_done"], n + 1)
                dve.tensor_tensor(kbmax[:, :], kmax[:, :], cols[:, NE:NE + 1], ALU.add).then_inc(s["kbmax_done"], 1)
                dve.wait_ge(s["kbmax_done"], n + 1)
                dve.tensor_tensor(kshift[:, :], cols[:, NE:NE + 1], kbmax[:, :], ALU.subtract).then_inc(s["kshift_ready"], 1)

            def q_bias(n):
                dve.wait_ge(s["qv_done"], n + 1)
                dve.tensor_tensor(qs[:, :, :].rearrange("p (t h) d -> p t (h d)", t=T), pQV[:, :, 0, :],
                                  bq_bc[:, :].unsqueeze(1).to_broadcast([P, T, P]), ALU.add).then_inc(s["qb_ready"], 1)

            def q_max(n):
                dve.wait_ge(s["qb_ready"], n + 1)
                dve.tensor_reduce(qmax[:, :], qs[:, :, :], AX.X, ALU.max).then_inc(s["qmax_done"], 1)

            def q_shift(n):
                dve.wait_ge(s["qmax_done"], n + 1)
                dve.tensor_tensor(qs[:, :, :], qs[:, :, :], qmax[:, :].unsqueeze(2).to_broadcast([P, T * HEADS, HEAD_DIM]),
                                  ALU.subtract).then_inc(s["qs_ready"], 1)

            def q_sum(n):
                dve.wait_ge(s["eq_ready"], n + 1)
                dve.tensor_reduce(qsum[:, :], eq[:, :, :], AX.X, ALU.add).then_inc(s["qsum_done"], 1)
                dve.wait_ge(s["qsum_done"], n + 1)
                dve.reciprocal(qinv[:, :], qsum[:, :]).then_inc(s["qinv_ready"], 1)

            def q_norm(n):
                dve.wait_ge(s["qinv_ready"], n + 1)
                dve.tensor_tensor(qn[:, :, :], eq[:, :, :], qinv[:, :].unsqueeze(2).to_broadcast([P, T * HEADS, HEAD_DIM]),
                                   ALU.mult).then_inc(s["qn_ready"], 1)

            def k_inv(n):
                dve.wait_ge(s["ek_exp"], n + 1)
                dve.reciprocal(kinv[:, :], ksum[:, :]).then_inc(s["kinv_ready"], 1)

            def state_out(n):
                dve.wait_ge(s["state_done"], n + 1)
                dve.wait_ge(s["kinv_ready"], n + 1)
                dve.scalar_tensor_tensor(out=s1[:, :], in0=pS, scalar=kinv[:, 0:1], in1=blockmask[:, :],
                                         op0=ALU.mult, op1=ALU.mult).then_inc(s["s1_done"], 1)
                dve.wait_ge(s["s1_done"], n + 1)
                dve.scalar_tensor_tensor(out=s2[:, :], in0=s1[:, :], scalar=1.0, in1=bv_mask[:, :], op0=ALU.mult, op1=ALU.add,
                                         accum_out=srow[:, :]).then_inc(s["s2_done"], 1)
                dve.wait_ge(s["s2_done"], n + 1)
                dve.tensor_scalar(smean[:, :], srow[:, :], -1.0 / C, None, ALU.mult).then_inc(s["smean_done"], 1)
                dve.wait_ge(s["smean_done"], n + 1)
                dve.tensor_scalar(s3[:, :], s2[:, :], smean[:, 0:1], None, ALU.add).then_inc(s["s_ready"], 1)

            def out_var(n):
                dve.wait_ge(s["ssq_done"], n + 1)
                dve.tensor_scalar(ve_o[:, :], pSSQ, 1.0 / C, LN_EPS, ALU.mult, ALU.add).then_inc(s["veo_done"], 1)

            def residual1(n):
                dve.wait_ge(s["wo_done"], n + 1)
                dve.wait_ge(s["rstdo_ready"], n + 1)
                dve.wait_ge(s["xg_ready"], n + 1)
                for t in range(T):
                    dve.scalar_tensor_tensor(out=x_all[:, n, t, :], in0=pC[:, t * P:(t + 1) * P], scalar=rstd_o[:, t:t + 1],
                                             in1=x_all[:, n, t, :], op0=ALU.mult, op1=ALU.add).then_inc(s["x1_ready"], 1)

            def x1_here(n):
                dve.wait_ge(s["x1_ready"], T * n + T)

            def ln2_stats(n):
                for t in range(T):
                    dve.bn_stats(st2[:, t, :], x_all[:, n, t, :]).then_inc(s["st2_done"], 1)

            def ln2_stats_here(n):
                dve.wait_ge(s["st2_done"], T * n + T)

            def ln2_var(n):
                for t in range(T):
                    dve.bn_aggr(mv2[:, t, :], st2[:, t, :]).then_inc(s["mv2_done"], 1)
                dve.wait_ge(s["mv2_done"], T * n + T)
                dve.tensor_scalar(ve2[:, :], mv2[:, :, 1], LN_EPS, None, ALU.add).then_inc(s["ve2_done"], 1)

            def ln2_apply(n):
                dve.wait_ge(s["rstd2_ready"], n + 1)
                w(dve, "h2T_done", n)
                for t in range(T):
                    dve.tensor_scalar(xn2[:, t, :], x_all[:, n, t, :], mv2[:, t, 0:1], rstd2[:, t:t + 1],
                                      ALU.subtract, ALU.mult).then_inc(s["xn2_ready"], 1)

            def route(n):
                dve.wait_ge(s["logits_done"], n + 1)
                dve.tensor_copy(lg[:, :, :].rearrange("p t e -> p (t e)"), pB[:, 0:T * NE]).then_inc(s["lg_ready"], 1)
                for t in range(T):
                    dve.max(top[:, t, :], pB[:, t * NE:(t + 1) * NE]).then_inc(s["top_done"], 1)
                dve.wait_ge(s["top_done"], T * n + T)
                dve.tensor_copy(top2[:, :, 0:2], top[:, :, 0:2]).then_inc(s["top2_done"], 1)
                dve.wait_ge(s["lg_ready"], n + 1)
                dve.wait_ge(s["top2_done"], n + 1)
                dve.tensor_tensor(lshift[:, :, :], lg[:, :, :], top[:, :, 0:1].to_broadcast([P, T, NE]),
                                  ALU.subtract).then_inc(s["lshift_ready"], 1)
                for t in range(T):
                    dve.match_replace(lg_cut[:, t, :], top2[:, t, :], lg[:, t, :], -3.0e38).then_inc(s["cut_done"], 1)

            def gates_out(n):
                dve.wait_ge(s["cut_done"], T * n + T)
                dve.tensor_tensor(chosen[:, :, :], lg[:, :, :], lg_cut[:, :, :], ALU.not_equal).then_inc(s["chosen_done"], 1)
                dve.wait_ge(s["elg_ready"], n + 1)
                dve.tensor_reduce(esum[:, :], elg[:, :, :], AX.X, ALU.add).then_inc(s["esum_done"], 1)
                dve.wait_ge(s["chosen_done"], n + 1)
                dve.tensor_tensor(echosen[:, :, :], elg[:, :, :], chosen[:, :, :], ALU.mult)
                dve.wait_ge(s["esum_done"], n + 1)
                dve.reciprocal(einv[:, :], esum[:, :]).then_inc(s["einv_done"], 1)
                dve.wait_ge(s["einv_done"], n + 1)
                w(dve, "gateT_done", n)
                gate = gate2[:, :, ROW:ROW + NE]
                dve.tensor_tensor(gate, echosen[:, :, :], einv[:, :].unsqueeze(2).to_broadcast([P, T, NE]),
                                  ALU.mult).then_inc(s["gate_done"], 1)
                dve.wait_ge(s["gate_done"], n + 1)
                dve.tensor_copy(gate_hi[:, :, :], gate).then_inc(s["ghi_done"], 1)
                dve.wait_ge(s["ghi_done"], n + 1)
                twice = lambda a: a.unsqueeze(2).to_broadcast([P, T, 2, NE])
                both = lambda k: gate2[:, :, 2 * NE * k:2 * NE * (k + 1)].rearrange("p t (w e) -> p t w e", w=2)
                dve.tensor_copy(both(0), twice(gate_hi[:, :, :].bitcast(F32)))
                dve.tensor_tensor(both(1), twice(gate), twice(gate_hi[:, :, :].bitcast(F32)), ALU.subtract).then_inc(s["gate2_ready"], 1)

            def weigh(b, par, e):
                dve.wait_ge(s["gelu_done"], NE * b + e + 1)
                dve.wait_ge(s[f"part{e * PARTS // NE}_{par}"], DMA // 2 * (b + 2 - par))
                w(dve, "mm2_done", NE * b + e - U + 1)
                dve.tensor_tensor(v[:, e % U, :], u[:, e % U, :], gate_bc[:, par, e, :], ALU.mult).then_inc(s["v_done"], 1)

            def v_low(b, e):
                dve.wait_ge(s["vhi_done"], fine_count(b, e))
                w(dve, "mm2_done", fine_before(b, e))
                i = FINE.index(e) % 2
                dve.tensor_tensor(v_lo[:, i, :], v[:, e % U, :], v_hi[:, i, :].bitcast(F32), ALU.subtract).then_inc(s["vlo_done"], 1)

            def residual2(b):
                dve.wait_ge(s["yT_done"], b + 1)
                xb = x_all[:, b, :, :]
                dve.tensor_tensor(xb, pB[:, :].rearrange("p (t c) -> p t c", t=T), xb, ALU.add).then_inc(s["out_ready"], 1)

            def step(b, par):
                Y, M, B, A2, A1, L = (has(b, k) for k in range(-1, 5))
                nxt = (par + 1) % 2
                if L:
                    x_here(b + 4)
                    ln1_stats(b + 4)
                if A2:
                    state_out(b + 2)
                if L:
                    ln1_stats_here(b + 4)
                if Y:
                    weigh(b - 1, nxt, 7)
                if L:
                    ln1_var(b + 4)
                if M:
                    weigh(b, par, 0)
                if A1:
                    k_max(b + 3)
                if L:
                    ln1_apply(b + 4)
                if M:
                    weigh(b, par, 2)
                if B:
                    route(b + 1)
                if A1:
                    q_bias(b + 3)
                    q_max(b + 3)
                    q_shift(b + 3)
                if A2:
                    out_var(b + 2)
                if B:
                    gates_out(b + 1)
                if A2:
                    residual1(b + 2)
                if Y:
                    residual2(b - 1)
                if A2:
                    x1_here(b + 2)
                if M:
                    weigh(b, par, 4)
                if A1:
                    q_sum(b + 3)
                    q_norm(b + 3)
                if A2:
                    ln2_stats(b + 2)
                    ln2_stats_here(b + 2)
                if A1:
                    k_inv(b + 3)
                if A2:
                    ln2_var(b + 2)
                if M:
                    v_low(b, 5)
                    weigh(b, par, 6)
                if A2:
                    ln2_apply(b + 2)
            run(dve, step, after={-4: attention_parts, -3: state_parts, -2: expert_parts})


_INS = ["L0_attn_x", "L0_attn_Wq", "L0_attn_bq", "L0_attn_Wk", "L0_attn_bk", "L0_attn_Wv", "L0_attn_bv", "L0_attn_Wo",
        "L0_attn_bo", "L0_attn_ln_g", "L0_attn_ln_b", "L0_ffn_router_w", "L0_ffn_w_in", "L0_ffn_b_in", "L0_ffn_w_out",
        "L0_ffn_b_out", "L0_c", "L0_wmod"]


def kernel(**inputs):
    import numpy as np
    import concourse.bacc as bacc
    from concourse.bass_utils import run_bass_kernel_spmd

    nc = bacc.Bacc("TRN2", target_bir_lowering=False, num_devices=1)
    arrays, args = {}, []
    for name in _INS:
        a = np.ascontiguousarray(inputs[name])
        arrays[f"in_{name}"] = a
        args.append(nc.dram_tensor(f"in_{name}", a.shape, mybir.dt.from_np(a.dtype), kind="ExternalInput").ap())
    x_shape = arrays["in_L0_attn_x"].shape
    out = nc.dram_tensor("out", x_shape, F32, kind="ExternalOutput").ap()
    gate_scratch = nc.dram_tensor("gate_scratch", (x_shape[0], 2 * P), F32, kind="Internal").ap()
    route_scratch = nc.dram_tensor("route_scratch", (2, arrays["in_L0_ffn_router_w"].shape[1], 4 * P), F32, kind="Internal").ap()
    adaln_block(nc, *args, out, gate_scratch, route_scratch)
    r = run_bass_kernel_spmd(nc, [arrays], core_ids=[0])
    return r.results[0]["out"]
```
